# Optimizing a Trainium2 kernel written in Bass

```python
import numpy as np
import jax
import jax.numpy as jnp

def _softmax(x, axis=-1):
    return jax.nn.softmax(x, axis=axis)
def _gelu(x):
    return jax.nn.gelu(x, approximate=True)
def _silu(x):
    return jax.nn.silu(x)
def _sigmoid(x):
    return jax.nn.sigmoid(x)
def _layernorm(x, axis=-1, eps=1e-5):
    m = jnp.mean(x, axis=axis, keepdims=True)
    v = jnp.var(x, axis=axis, keepdims=True)
    return (x - m) / jnp.sqrt(v + eps)
def _scatter_add(tgt, idx, src, axis=0):
    return tgt.at[idx].add(src)
def _segment_sum(src, seg, n):
    return jax.ops.segment_sum(src, seg, n)

kernel_name = 'mk_conv_preact_d2_conv_nchw96_10e7d9'

def setup_inputs(seed: int = 0):
    np.random.seed(seed)
    _w = jnp.asarray
    def _rec_inputs():
        import jax
        import jax.numpy as jnp
        _gk = jax.random.key(seed)
        x = -0.0004039 + 1 * jax.random.normal(jax.random.fold_in(_gk, 1), (2, 96, 256, 256), jnp.float32)
        return x
    x = _rec_inputs()
    def _L0_conv_setup():
        import jax, jax.numpy as jnp
        import numpy as np
        from functools import partial
        EPS = 1e-05

        def _positions(size, step, ps):
            pos = []
            for i in range(0, size + step - ps, step):
                t = i
                if i + ps > size:
                    t = size - ps
                pos.append(t)
            return np.asarray(pos, dtype=np.int32)

        def _div_factor(size, step, ps):
            f = np.ones(size, dtype=np.float32)
            for i in range(step, size + step - ps, step):
                top, down = (i, i + ps - step)
                if top + ps > size:
                    top = size - ps
                f[top:down] *= 0.5
            return f

        def _layernorm(x, w, b):
            m = jnp.mean(x, axis=-1, keepdims=True)
            v = jnp.var(x, axis=-1, keepdims=True)
            return (x - m) / jnp.sqrt(v + EPS) * w + b

        def _gelu(x):
            return jax.nn.gelu(x, approximate=False)
        HEADS = 4
        key = jax.random.key(seed)
        ks = jax.random.split(key, 8)
        dim, qk_dim, mlp_dim = (96, 64, 192)
        b, h, w = (2, 256, 256)
        s = lambda fan: 1.0 / np.sqrt(fan)
        return {'x': jax.random.normal(ks[0], (b, dim, h, w), jnp.float32), 'norm1_w': jnp.ones((dim,), jnp.float32), 'norm1_b': jnp.zeros((dim,), jnp.float32), 'wq': jax.random.normal(ks[1], (dim, qk_dim), jnp.float32) * s(dim), 'wk': jax.random.normal(ks[2], (dim, qk_dim), jnp.float32) * s(dim), 'wv': jax.random.normal(ks[3], (dim, dim), jnp.float32) * s(dim), 'wproj': jax.random.normal(ks[4], (dim, dim), jnp.float32) * s(dim), 'norm2_w': jnp.ones((dim,), jnp.float32), 'norm2_b': jnp.zeros((dim,), jnp.float32), 'fc1_w': jax.random.normal(ks[5], (dim, mlp_dim), jnp.float32) * s(dim), 'fc1_b': jnp.zeros((mlp_dim,), jnp.float32), 'dw_w': jax.random.normal(ks[6], (mlp_dim, 1, 5, 5), jnp.float32) * s(25), 'dw_b': jnp.zeros((mlp_dim,), jnp.float32), 'fc2_w': jax.random.normal(ks[7], (mlp_dim, dim), jnp.float32) * s(mlp_dim), 'fc2_b': jnp.zeros((dim,), jnp.float32), 'ps': 16}
    _L0_conv_all = _L0_conv_setup()
    _L0_conv_in = {k: v for k, v in _L0_conv_all.items() if k in ('norm1_w', 'norm1_b', 'wq', 'wk', 'wv', 'wproj', 'norm2_w', 'norm2_b', 'fc1_w', 'fc1_b', 'dw_w', 'dw_b', 'fc2_w', 'fc2_b', )}
    del _L0_conv_all

    def _L1_conv_setup():
        import jax, jax.numpy as jnp
        import numpy as np
        HEADS, HEAD_DIM = (8, 32)
        FOLD_W = FOLD_H = 8
        PW = PH = 2

        def _l2norm(t):
            n = jnp.maximum(jnp.linalg.norm(t, axis=-1, keepdims=True), 1e-12)
            return t / n

        def _cluster_forward(x, Wf, bf, Wv, bv, Wp, bp, sim_alpha, sim_beta):
            B, C, W, H = x.shape
            v = jnp.einsum('bchw,oc->bohw', x, Wv) + bv[None, :, None, None]
            f = jnp.einsum('bchw,oc->bohw', x, Wf) + bf[None, :, None, None]

            def split_heads(t):
                b = t.shape[0]
                return t.reshape(b, HEADS, HEAD_DIM, W, H).reshape(b * HEADS, HEAD_DIM, W, H)
            f, v = (split_heads(f), split_heads(v))

            def fold(t):
                b, c, w0, h0 = t.shape
                ws, hs = (w0 // FOLD_W, h0 // FOLD_H)
                t = t.reshape(b, c, FOLD_W, ws, FOLD_H, hs)
                return t.transpose(0, 2, 4, 1, 3, 5).reshape(b * FOLD_W * FOLD_H, c, ws, hs)
            f, v = (fold(f), fold(v))
            b, c, w, h = f.shape

            def pool(t):
                return t.reshape(b, c, PW, w // PW, PH, h // PH).max(axis=(3, 5))
            centers = pool(f).reshape(b, c, PW * PH).transpose(0, 2, 1)
            value_centers = pool(v).reshape(b, c, PW * PH).transpose(0, 2, 1)
            pts = f.reshape(b, c, w * h).transpose(0, 2, 1)
            cos = jnp.einsum('bmc,bnc->bmn', _l2norm(centers), _l2norm(pts))
            sim = jax.nn.sigmoid(sim_beta + sim_alpha * cos)
            idx = jnp.argmax(sim, axis=1)
            mask = jax.nn.one_hot(idx, sim.shape[1], dtype=sim.dtype)
            mask = jnp.transpose(mask, (0, 2, 1))
            sim = sim * mask
            value2 = v.reshape(b, c, w * h).transpose(0, 2, 1)
            agg = (jnp.einsum('bnc,bmn->bmc', value2, sim) + value_centers) / (mask.sum(axis=-1, keepdims=True) + 1.0)
            out = jnp.einsum('bmc,bmn->bnc', agg, sim)
            out = out.transpose(0, 2, 1).reshape(b, c, w, h)
            bb = b // (FOLD_W * FOLD_H)
            out = out.reshape(bb, FOLD_W, FOLD_H, c, w, h).transpose(0, 3, 1, 4, 2, 5)
            out = out.reshape(bb, c, FOLD_W * w, FOLD_H * h)
            out = out.reshape(bb // HEADS, HEADS * HEAD_DIM, W, H)
            out = jnp.einsum('bchw,oc->bohw', out, Wp) + bp[None, :, None, None]
            return out
        key = jax.random.key(seed)
        ks = jax.random.split(key, 8)
        dim, hd = (96, HEADS * HEAD_DIM)
        return {'x': jax.random.normal(ks[0], (16, dim, 64, 64), jnp.float32), 'Wf': jax.random.normal(ks[1], (hd, dim), jnp.float32) * 0.05, 'bf': jax.random.normal(ks[2], (hd,), jnp.float32) * 0.01, 'Wv': jax.random.normal(ks[3], (hd, dim), jnp.float32) * 0.05, 'bv': jax.random.normal(ks[4], (hd,), jnp.float32) * 0.01, 'Wp': jax.random.normal(ks[5], (dim, hd), jnp.float32) * 0.05, 'bp': jax.random.normal(ks[6], (dim,), jnp.float32) * 0.01, 'sim_alpha': jnp.ones((1,), jnp.float32), 'sim_beta': jnp.zeros((1,), jnp.float32)}
    _L1_conv_all = _L1_conv_setup()
    _L1_conv_in = {k: v for k, v in _L1_conv_all.items() if k in ('Wf', 'bf', 'Wv', 'bv', 'Wp', 'bp', 'sim_alpha', 'sim_beta', )}
    del _L1_conv_all

    return {
        "x": x,
        "L0_conv_norm1_w": _L0_conv_in["norm1_w"],
        "L0_conv_norm1_b": _L0_conv_in["norm1_b"],
        "L0_conv_wq": _L0_conv_in["wq"],
        "L0_conv_wk": _L0_conv_in["wk"],
        "L0_conv_wv": _L0_conv_in["wv"],
        "L0_conv_wproj": _L0_conv_in["wproj"],
        "L0_conv_norm2_w": _L0_conv_in["norm2_w"],
        "L0_conv_norm2_b": _L0_conv_in["norm2_b"],
        "L0_conv_fc1_w": _L0_conv_in["fc1_w"],
        "L0_conv_fc1_b": _L0_conv_in["fc1_b"],
        "L0_conv_dw_w": _L0_conv_in["dw_w"],
        "L0_conv_dw_b": _L0_conv_in["dw_b"],
        "L0_conv_fc2_w": _L0_conv_in["fc2_w"],
        "L0_conv_fc2_b": _L0_conv_in["fc2_b"],
        "L1_conv_Wf": _L1_conv_in["Wf"],
        "L1_conv_bf": _L1_conv_in["bf"],
        "L1_conv_Wv": _L1_conv_in["Wv"],
        "L1_conv_bv": _L1_conv_in["bv"],
        "L1_conv_Wp": _L1_conv_in["Wp"],
        "L1_conv_bp": _L1_conv_in["bp"],
        "L1_conv_sim_alpha": _L1_conv_in["sim_alpha"],
        "L1_conv_sim_beta": _L1_conv_in["sim_beta"],
    }

def reference(x, L0_conv_norm1_w, L0_conv_norm1_b, L0_conv_wq, L0_conv_wk, L0_conv_wv, L0_conv_wproj, L0_conv_norm2_w, L0_conv_norm2_b, L0_conv_fc1_w, L0_conv_fc1_b, L0_conv_dw_w, L0_conv_dw_b, L0_conv_fc2_w, L0_conv_fc2_b, L1_conv_Wf, L1_conv_bf, L1_conv_Wv, L1_conv_bv, L1_conv_Wp, L1_conv_bp, L1_conv_sim_alpha, L1_conv_sim_beta):
    import jax
    import jax.numpy as jnp
    def _L0_conv_ref(x, norm1_w, norm1_b, wq, wk, wv, wproj, norm2_w, norm2_b, fc1_w, fc1_b, dw_w, dw_b, fc2_w, fc2_b, ps):
        import jax, jax.numpy as jnp
        import numpy as np
        from functools import partial
        EPS = 1e-05

        def _positions(size, step, ps):
            pos = []
            for i in range(0, size + step - ps, step):
                t = i
                if i + ps > size:
                    t = size - ps
                pos.append(t)
            return np.asarray(pos, dtype=np.int32)

        def _div_factor(size, step, ps):
            f = np.ones(size, dtype=np.float32)
            for i in range(step, size + step - ps, step):
                top, down = (i, i + ps - step)
                if top + ps > size:
                    top = size - ps
                f[top:down] *= 0.5
            return f

        def _layernorm(x, w, b):
            m = jnp.mean(x, axis=-1, keepdims=True)
            v = jnp.var(x, axis=-1, keepdims=True)
            return (x - m) / jnp.sqrt(v + EPS) * w + b

        def _gelu(x):
            return jax.nn.gelu(x, approximate=False)
        HEADS = 4
        b, c, h, w = x.shape
        step = ps - 2
        if h == ps and w == ps:
            step = ps
        tops = _positions(h, step, ps)
        lefts = _positions(w, step, ps)
        nh, nw = (len(tops), len(lefts))
        n = nh * nw
        row_idx = tops[:, None] + np.arange(ps)
        col_idx = lefts[:, None] + np.arange(ps)
        crop = x[:, :, row_idx[:, None, :, None], col_idx[None, :, None, :]]
        tok = crop.transpose(0, 2, 3, 4, 5, 1).reshape(b * n, ps * ps, c)
        y = _layernorm(tok, norm1_w, norm1_b)
        qk_dim = wq.shape[1]
        hd_q = qk_dim // HEADS
        hd_v = c // HEADS
        q = (y @ wq).reshape(b * n, ps * ps, HEADS, hd_q).transpose(0, 2, 1, 3)
        k = (y @ wk).reshape(b * n, ps * ps, HEADS, hd_q).transpose(0, 2, 1, 3)
        v = (y @ wv).reshape(b * n, ps * ps, HEADS, hd_v).transpose(0, 2, 1, 3)
        scores = jnp.einsum('bhnd,bhmd->bhnm', q, k) / jnp.sqrt(jnp.float32(hd_q))
        attn = jax.nn.softmax(scores, axis=-1)
        out = jnp.einsum('bhnm,bhmd->bhnd', attn, v)
        out = out.transpose(0, 2, 1, 3).reshape(b * n, ps * ps, c)
        tok = out @ wproj + tok
        crop = tok.reshape(b, nh, nw, ps, ps, c).transpose(0, 5, 1, 2, 3, 4)
        acc = jnp.zeros_like(x)
        acc = acc.at[:, :, row_idx[:, None, :, None], col_idx[None, :, None, :]].add(crop)
        fh = jnp.asarray(_div_factor(h, step, ps))
        fw = jnp.asarray(_div_factor(w, step, ps))
        x2 = acc * fh[None, None, :, None] * fw[None, None, None, :]
        tok2 = x2.transpose(0, 2, 3, 1).reshape(b, h * w, c)
        y = _layernorm(tok2, norm2_w, norm2_b)
        y = _gelu(y @ fc1_w + fc1_b)
        mlp = y.shape[-1]
        ymap = y.transpose(0, 2, 1).reshape(b, mlp, h, w)
        dw = jax.lax.conv_general_dilated(ymap, dw_w, window_strides=(1, 1), padding=((2, 2), (2, 2)), dimension_numbers=('NCHW', 'OIHW', 'NCHW'), feature_group_count=mlp)
        dw = _gelu(dw + dw_b[None, :, None, None])
        y = y + dw.reshape(b, mlp, h * w).transpose(0, 2, 1)
        tok2 = y @ fc2_w + fc2_b + tok2
        return tok2.reshape(b, h, w, c).transpose(0, 3, 1, 2)

    def _L1_conv_ref(x, Wf, bf, Wv, bv, Wp, bp, sim_alpha, sim_beta):
        import jax, jax.numpy as jnp
        import numpy as np
        HEADS, HEAD_DIM = (8, 32)
        FOLD_W = FOLD_H = 8
        PW = PH = 2

        def _l2norm(t):
            n = jnp.maximum(jnp.linalg.norm(t, axis=-1, keepdims=True), 1e-12)
            return t / n

        def _cluster_forward(x, Wf, bf, Wv, bv, Wp, bp, sim_alpha, sim_beta):
            B, C, W, H = x.shape
            v = jnp.einsum('bchw,oc->bohw', x, Wv) + bv[None, :, None, None]
            f = jnp.einsum('bchw,oc->bohw', x, Wf) + bf[None, :, None, None]

            def split_heads(t):
                b = t.shape[0]
                return t.reshape(b, HEADS, HEAD_DIM, W, H).reshape(b * HEADS, HEAD_DIM, W, H)
            f, v = (split_heads(f), split_heads(v))

            def fold(t):
                b, c, w0, h0 = t.shape
                ws, hs = (w0 // FOLD_W, h0 // FOLD_H)
                t = t.reshape(b, c, FOLD_W, ws, FOLD_H, hs)
                return t.transpose(0, 2, 4, 1, 3, 5).reshape(b * FOLD_W * FOLD_H, c, ws, hs)
            f, v = (fold(f), fold(v))
            b, c, w, h = f.shape

            def pool(t):
                return t.reshape(b, c, PW, w // PW, PH, h // PH).max(axis=(3, 5))
            centers = pool(f).reshape(b, c, PW * PH).transpose(0, 2, 1)
            value_centers = pool(v).reshape(b, c, PW * PH).transpose(0, 2, 1)
            pts = f.reshape(b, c, w * h).transpose(0, 2, 1)
            cos = jnp.einsum('bmc,bnc->bmn', _l2norm(centers), _l2norm(pts))
            sim = jax.nn.sigmoid(sim_beta + sim_alpha * cos)
            idx = jnp.argmax(sim, axis=1)
            mask = jax.nn.one_hot(idx, sim.shape[1], dtype=sim.dtype)
            mask = jnp.transpose(mask, (0, 2, 1))
            sim = sim * mask
            value2 = v.reshape(b, c, w * h).transpose(0, 2, 1)
            agg = (jnp.einsum('bnc,bmn->bmc', value2, sim) + value_centers) / (mask.sum(axis=-1, keepdims=True) + 1.0)
            out = jnp.einsum('bmc,bmn->bnc', agg, sim)
            out = out.transpose(0, 2, 1).reshape(b, c, w, h)
            bb = b // (FOLD_W * FOLD_H)
            out = out.reshape(bb, FOLD_W, FOLD_H, c, w, h).transpose(0, 3, 1, 4, 2, 5)
            out = out.reshape(bb, c, FOLD_W * w, FOLD_H * h)
            out = out.reshape(bb // HEADS, HEADS * HEAD_DIM, W, H)
            out = jnp.einsum('bchw,oc->bohw', out, Wp) + bp[None, :, None, None]
            return out
        return _cluster_forward(x, Wf, bf, Wv, bv, Wp, bp, sim_alpha, sim_beta)

    def _gn(v, G=32, eps=1e-5):
        B_, C_, H_, W_ = v.shape
        g = v.reshape(B_, G, C_ // G, H_, W_)
        m = jnp.mean(g, axis=(2, 3, 4), keepdims=True)
        s = jnp.var(g, axis=(2, 3, 4), keepdims=True)
        return ((g - m) / jnp.sqrt(s + eps)).reshape(v.shape)

    def _ln_c(v, eps=1e-6):
        m = jnp.mean(v, axis=1, keepdims=True)
        s = jnp.var(v, axis=1, keepdims=True)
        return (v - m) / jnp.sqrt(s + eps)

    def _ln_t(v, eps=1e-5):
        m = jnp.mean(v, axis=-1, keepdims=True)
        s = jnp.var(v, axis=-1, keepdims=True)
        return (v - m) / jnp.sqrt(s + eps)

    def _to_tokens(v):
        B_, C_, H_, W_ = v.shape
        return v.reshape(B_, C_, H_ * W_).transpose(0, 2, 1)
    def _from_tokens(t, like):
        B_, C_, H_, W_ = like.shape
        return t.transpose(0, 2, 1).reshape(B_, C_, H_, W_)

    x = x + _L0_conv_ref(_gn(x), L0_conv_norm1_w, L0_conv_norm1_b, L0_conv_wq, L0_conv_wk, L0_conv_wv, L0_conv_wproj, L0_conv_norm2_w, L0_conv_norm2_b, L0_conv_fc1_w, L0_conv_fc1_b, L0_conv_dw_w, L0_conv_dw_b, L0_conv_fc2_w, L0_conv_fc2_b, 16)
    x = x + _L1_conv_ref(_gn(x), L1_conv_Wf, L1_conv_bf, L1_conv_Wv, L1_conv_bv, L1_conv_Wp, L1_conv_bp, L1_conv_sim_alpha, L1_conv_sim_beta)
    return x


_drawn_inputs = setup_inputs


def setup_inputs(seed=0):
    import zlib

    import numpy as np

    out = dict(_drawn_inputs(seed))
    spreads = {'L0_conv_norm1_w': (1.0, 0.2),
     'L0_conv_norm1_b': (0.0, 0.1),
     'L0_conv_norm2_w': (1.0, 0.2),
     'L0_conv_norm2_b': (0.0, 0.1),
     'L0_conv_fc1_b': (0.0, 0.1),
     'L0_conv_dw_b': (0.0, 0.1),
     'L0_conv_fc2_b': (0.0, 0.1)}
    factors = {'L1_conv_Wf': 8.0,
     'L1_conv_bf': 26.261,
     'L1_conv_Wv': 4.27,
     'L1_conv_bv': 8.0,
     'L1_conv_Wp': 4.291,
     'L1_conv_bp': 8.0}
    for name, (base, spread) in spreads.items():
        noise = np.random.default_rng([zlib.crc32(name.encode()), seed]).standard_normal(out[name].shape)
        drawn = base * np.exp(spread * noise) if base else spread * noise
        out[name] = jnp.asarray(drawn.astype(out[name].dtype))
    for name, factor in factors.items():
        out[name] = (out[name] * factor).astype(out[name].dtype)
    return out
```

```python
from contextlib import ExitStack

import numpy as np

import concourse.bass as bass
from concourse import mybir

F32 = mybir.dt.float32
BF16 = mybir.dt.bfloat16
ALU = mybir.AluOpType
ACT = mybir.ActivationFunctionType
AX = mybir.AxisListType

B, C, H, W = 2, 96, 256, 256
HW = H * W
P = 128
T = 512
GROUP = C // 32
EPS = 1e-5
EPS0 = 1e-5

PS, STEP = 16, 14
NSTRIP = (H + STEP - PS - 1) // STEP + 1
LAST = H - PS
HEADS, DQ, DV = 4, 16, 24
QK = HEADS * DQ
VW = 32
MLP = 192
KS, PAD = 5, 2
WP = W + 2 * PAD
TAB = 260

H1, D1, NC1 = 8, 32, 4
HD = H1 * D1
BS = 32


def constants():
    ident = np.eye(P, dtype=np.float32)
    groups = np.zeros((C, C), np.float32)
    for g in range(0, C, GROUP):
        groups[g:g + GROUP, g:g + GROUP] = 1.0 / GROUP
    centre = (np.eye(C) - np.full((C, C), 1.0 / C)).astype(np.float32)
    mean = np.full((C, C), 1.0 / C, np.float32)
    denom = np.zeros((P, P), np.float32)
    for h in range(HEADS):
        denom[h * VW + DV, h * VW:(h + 1) * VW] = 1.0
    channel, feature = np.arange(P), np.arange(HD)
    same = (channel[:, None] // D1 == channel[None] // D1).astype(np.float32)
    headc = (feature[:, None] // D1 == np.arange(H1 * NC1)[None] // NC1).astype(np.float32)
    headc = np.ascontiguousarray(headc.reshape(HD // P, P, -1).transpose(1, 0, 2))
    first = np.broadcast_to(np.arange(NC1, 0, -1, dtype=np.float32), (P, 64, NC1)).copy()
    return dict(c_same=same, c_headc=headc, c_first=first, c_ident=ident, c_groups=groups, c_centre=centre, c_mean=mean, c_denom=denom)


class Env:
    pass


def stack_count(t, m, unroll):
    return (t - m + unroll) // unroll


def after(eng, s, per, t, k=0):
    v = t * per + k
    if not isinstance(v, int) or v > 0:
        eng.wait_ge(s, v)


def pipeline(eng, n, unroll, ahead, behind, step, peel=1):
    first, start = -ahead, max(behind, peel)
    loops = (n - ahead - start) // unroll

    def some(t):
        step(t, t % unroll, lambda k: 0 <= k < n)

    for t in range(first, start):
        some(t)
    if loops:
        with eng.Fori(0, loops) as i:
            for k in range(unroll):
                step(i * unroll + (start + k), (start + k) % unroll, lambda p: True)
    for t in range(start + loops * unroll, n + behind):
        some(t)


def column(ap):
    return ap.rearrange("(c o) -> c o", o=1)


def stage_stats(nc, e, src, tag):
    ROWS = 16
    N = ROWS * W
    CH = H // ROWS
    SUB = N // T
    with ExitStack() as ctx:
        xin = ctx.enter_context(nc.sbuf_tensor(f"{tag}_xin", [C, 2, N], F32))
        loaded = [ctx.enter_context(nc.semaphore(f"{tag}_loaded{k}")) for k in range(2)]
        used = ctx.enter_context(nc.semaphore(f"{tag}_used"))
        block = ctx.enter_context(nc.Block())

        @block.sync
        def _(sp):
            for b in range(B):
                with sp.Fori(0, CH // 2) as i:
                    for k in range(2):
                        sp.wait_ge(used, 2 * i + (b * CH + k + 1))
                        sp.dma_start(
                            xin[:, k, :].rearrange("c (o n) -> c o n", o=1),
                            src[b].rearrange("c (k n) -> c k n", n=N)[:, bass.ds(2 * i + k, 1), :],
                        ).then_inc(loaded[k], 16)

        @block.vector
        def _(dve):
            dve.nop().then_inc(used, 2)
            with dve.Fori(0, B * CH // 2) as i:
                for k in range(2):
                    dve.wait_ge(loaded[k], 16 * i + 16)
                    for s in range(SUB):
                        last = nc.vector.bn_stats(
                            e.moments[:, bass.ds(((2 * i + k) * SUB + s) * 6, 6)], xin[:, k, s * T:(s + 1) * T])
                    last.then_inc(used, 1)


def stage_affine(nc, e, gain, shift, tag):
    NT = HW // T
    with ExitStack() as ctx:
        def sb(name, shape):
            return ctx.enter_context(nc.sbuf_tensor(f"{tag}_{name}", shape, F32))
        mv = sb("mv", [C, B, 2])
        diff = sb("diff", [C, B])
        spread = sb("spread", [C, B])
        gmean = sb("gmean", [C, B])
        std = sb("std", [C, B])
        pm = ctx.enter_context(nc.psum_tensor(f"{tag}_pm", [C, 2, T], F32))
        done = ctx.enter_context(nc.semaphore(f"{tag}_done"))
        rooted = ctx.enter_context(nc.semaphore(f"{tag}_rooted"))
        summed = ctx.enter_context(nc.semaphore(f"{tag}_summed"))
        block = ctx.enter_context(nc.Block())

        @block.vector
        def _(dve):
            for b in range(B):
                nc.vector.bn_aggr(mv[:, b, :], e.moments[:, b * NT * 6:(b + 1) * NT * 6]).then_inc(done, 1)
            dve.wait_ge(summed, 1)
            nc.vector.tensor_copy(gmean[:], pm[:, 0, 0:B]).then_inc(done, 1)
            dve.wait_ge(done, 3)
            nc.vector.tensor_tensor(diff[:], mv[:, :, 0], gmean[:], ALU.subtract).then_inc(done, 1)
            dve.wait_ge(done, 4)
            nc.vector.tensor_tensor(spread[:], diff[:], diff[:], ALU.mult).then_inc(done, 1)
            dve.wait_ge(done, 5)
            nc.vector.tensor_tensor(spread[:], spread[:], mv[:, :, 1], ALU.add).then_inc(done, 1)
            dve.wait_ge(rooted, 1)
            nc.vector.reciprocal(gain[:], std[:]).then_inc(done, 1)
            dve.wait_ge(done, 7)
            nc.vector.scalar_tensor_tensor(out=shift[:], in0=gmean[:], scalar=-1.0, in1=gain[:],
                                           op0=ALU.mult, op1=ALU.mult).then_inc(done, 1)

        @block.tensor
        def _(pe):
            pe.wait_ge(done, 2)
            nc.tensor.matmul(pm[:, 0, 0:B], e.groups[:], mv[:, :, 0], start=True, stop=True).then_inc(summed, 1)
            pe.wait_ge(done, 6)
            nc.tensor.matmul(pm[:, 1, 0:B], e.groups[:], spread[:], start=True, stop=True).then_inc(summed, 1)

        @block.scalar
        def _(act):
            act.wait_ge(summed, 2)
            nc.scalar.activation(std[:], pm[:, 1, 0:B], ACT.Sqrt, bias=e.eps[0:C, :]).then_inc(rooted, 1)


def stage_norm1(nc, e):
    U = 2
    NT = 4
    N = NT * T
    CH = HW // N
    LAG = 1
    with ExitStack() as ctx:
        def sb(name, shape):
            return ctx.enter_context(nc.sbuf_tensor(f"n1_{name}", shape, F32))

        def sem(name):
            return ctx.enter_context(nc.semaphore(f"n1_{name}"))

        xin, yout = sb("xin", [C, U, N]), sb("yout", [C, U, N])
        sq, rstd = sb("sq", [C, NT, T]), sb("rstd", [C, NT, T])
        wc = sb("wc", [C, B, C])
        bc = sb("bc", [C, B])
        pc = ctx.enter_context(nc.psum_tensor("n1_pc", [C, NT, T], F32))
        pv = ctx.enter_context(nc.psum_tensor("n1_pv", [C, NT, T], F32))
        loaded = [sem(f"loaded{m}") for m in range(U)]
        stored = [sem(f"stored{m}") for m in range(U)]
        prep, prepmm = sem("prep"), sem("prepmm")
        centred, squared, varied, logged, inverted, normed = (
            sem(n) for n in ("centred", "squared", "varied", "logged", "inverted", "normed"))
        block = ctx.enter_context(nc.Block())

        def tiles(t, g, m, has, early, late):
            for s in range(NT):
                if has(t):
                    early(g, m, s)
                if s < LAG and has(t - 1):
                    late(g - 1, (m - 1) % U, s + NT - LAG)
                if s >= LAG and has(t):
                    late(g, m, s - LAG)

        @block.sync
        def _(sp):
            for b in range(B):
                def step(t, m, has):
                    g = t + b * CH
                    if has(t + U):
                        after(sp, centred, NT, g, NT)
                        sp.dma_start(xin[:, m, :], e.x[b][:, bass.ds((t + U) * N, N)]).then_inc(loaded[m], 16)
                    if has(t - 1):
                        o = (m - 1) % U
                        after(sp, normed, NT, g - 1, NT)
                        sp.dma_start(e.y[b][:, bass.ds((t - 1) * N, N)], yout[:, o, :]).then_inc(stored[o], 16)
                pipeline(sp, CH, U, U, 1, step)
            for m in range(U):
                sp.wait_ge(stored[m], 16 * (B * CH // U))

        @block.tensor
        def _(pe):
            for b in range(B):
                nc.tensor.matmul(pv[:, b, 0:1], e.centre[:], e.shift0[:, b:b + 1], start=True, stop=True).then_inc(prepmm, 1)
            pe.wait_ge(prep, B + B)
            for b in range(B):
                def centre(g, m, s):
                    pe.wait_ge(loaded[m], 16 * stack_count(g, m, U))
                    after(pe, normed, NT, g - 1, s + 1)
                    nc.tensor.matmul(pc[:, s, :], wc[:, b, :], xin[:, m, s * T:(s + 1) * T],
                                     start=True, stop=True).then_inc(centred, 1)

                def vary(g, m, s):
                    after(pe, squared, NT, g, s + 1)
                    after(pe, logged, NT, g - 1, s + 1)
                    nc.tensor.matmul(pv[:, s, :], e.mean[:], sq[:, s, :], start=True, stop=True).then_inc(varied, 1)

                def step(t, m, has):
                    tiles(t, t + b * CH, m, has, centre, vary)
                pipeline(pe, CH, U, 0, 1, step)

        @block.scalar
        def _(act):
            act.preload_act_table_set("natural_log_exp_and_others")
            act.wait_ge(prep, B + B)
            for b in range(B):
                def square(g, m, s):
                    after(act, centred, NT, g, s + 1)
                    after(act, varied, NT, g - 1, s + 1)
                    nc.scalar.activation(sq[:, s, :], pc[:, s, :], ACT.Square, bias=bc[:, b:b + 1]).then_inc(squared, 1)

                def invert(g, m, s):
                    after(act, varied, NT, g, s + 1)
                    after(act, normed, NT, g - 1, s + 1)
                    nc.scalar.activation(rstd[:, s, :], pv[:, s, :], ACT.Ln, bias=e.eps[0:C, :]).then_inc(logged, 1)
                    after(act, logged, NT, g, s + 1)
                    nc.scalar.activation(rstd[:, s, :], rstd[:, s, :], ACT.Exp, scale=-0.5).then_inc(inverted, 1)

                def step(t, m, has):
                    tiles(t, t + b * CH, m, has, square, invert)
                pipeline(act, CH, U, 0, 1, step)

        @block.vector
        def _(dve):
            for b in range(B):
                nc.vector.tensor_scalar(wc[:, b, :], e.centre[:], e.gain0[:, b:b + 1], None, ALU.mult).then_inc(prep, 1)
            dve.wait_ge(prepmm, B)
            for b in range(B):
                nc.vector.tensor_copy(bc[:, b:b + 1], pv[:, b, 0:1]).then_inc(prep, 1)
            dve.wait_ge(prep, B + B)
            for b in range(B):
                g0 = b * CH

                def step(t, m, has):
                    if not has(t):
                        return
                    g = t + g0
                    if has(t - U) or g0:
                        dve.wait_ge(stored[m], 16 * stack_count(g - U, m, U))
                    for s in range(NT):
                        after(dve, inverted, NT, g, s + 1)
                        nc.vector.scalar_tensor_tensor(
                            out=yout[:, m, s * T:(s + 1) * T], in0=pc[:, s, :], scalar=bc[:, b:b + 1],
                            in1=rstd[:, s, :], op0=ALU.add, op1=ALU.mult).then_inc(normed, 1)
                pipeline(dve, CH, U, 0, U, step)


def stage_attend(nc, e):
    NP = NSTRIP * NSTRIP
    NW = NSTRIP
    TOK = PS * PS
    T2 = B * TOK
    KQ = 6 * DQ
    KM = KQ + 2
    U = 4
    SC = PS * W
    with ExitStack() as ctx:
        def sb(name, shape, dt=F32):
            return ctx.enter_context(nc.sbuf_tensor(f"at_{name}", shape, dt))

        def sem(name):
            return ctx.enter_context(nc.semaphore(f"at_{name}"))

        ys = sb("ys", [C + 1, 2, B, PS, W])
        av = sb("av", [C, 2, B * PS, W])
        xw = sb("xw", [C + 1, 2, T2])
        wqk = sb("wqk", [C + 1, 2 * QK])
        wv = sb("wv", [C + 1, HEADS, VW])
        wp = sb("wp", [P, C])
        w_in = sb("w_in", [C, 2 * QK + C])
        n1w, n1b = sb("n1w", [C, 1]), sb("n1b", [C, 1])
        denom = sb("denom", [P, P])
        half = sb("half", [C, 1])
        rest = sb("rest", [P, T2])
        parts = sb("parts", [P, 2, 3, T2], BF16)
        qs = sb("qs", [KM, U, HEADS, T2], BF16)
        ks = sb("ks", [KM, U, HEADS, T2], BF16)
        vs = sb("vs", [P, U, B * 2, P])
        mx = sb("mx", [P, HEADS, B * 2])
        nmx = sb("nmx", [P, 2, HEADS, B * 2], BF16)
        identb = sb("identb", [P, P], BF16)
        nmt = sb("nmt", [2 * HEADS * B * 2, P], BF16)
        pr = sb("pr", [P, 4, 2, 2, TOK])
        os_ = sb("os", [P, T2])
        rcp = sb("rcp", [P, T2])
        pw = sb("pw", [C, T2])
        psS = ctx.enter_context(nc.psum_tensor("at_psS", [P, 2, T], F32))
        psT = ctx.enter_context(nc.psum_tensor("at_psT", [P, 2, 2, T], F32))
        psO = ctx.enter_context(nc.psum_tensor("at_psO", [P, T], F32))
        psM = ctx.enter_context(nc.psum_tensor("at_psM", [P, T], F32))

        w_loaded, w_done, w_bias, ready = sem("w_loaded"), sem("w_done"), sem("w_bias"), sem("ready")
        y_in, staged, a_out = sem("y_in"), sem("staged"), sem("a_out")
        qk_mm, qk_hi, qk_rest, qk_mid, qk_lo = (sem(n) for n in ("qk_mm", "qk_hi", "qk_rest", "qk_mid", "qk_lo"))
        stacked = [sem(f"stacked{m}") for m in range(U)]
        v_mm, v_sb, s_mm, s_max = sem("v_mm"), sem("v_sb"), sem("s_mm"), sem("s_max")
        nm1, nm2, nmt_mm, nmt_sb = sem("nm1"), sem("nm2"), sem("nmt_mm"), sem("nmt_sb")
        maxrow = [sem(f"maxrow{m}") for m in range(U)]
        t_mm, t_exp, pv_mm, o_sb, d_mm, d_ln, d_rcp, o_n, p_mm, p_sb, acc, fin = (
            sem(n) for n in ("t_mm", "t_exp", "pv_mm", "o_sb", "d_mm", "d_ln", "d_rcp", "o_n", "p_mm", "p_sb", "acc", "fin"))
        a = e.aps
        y4 = e.y.rearrange("b c n -> c b n")
        a4 = e.attn.rearrange("b c n -> c b n")
        block = ctx.enter_context(nc.Block())


        @block.sync
        def _(sp):
            wsrc = ((w_in[:, 0:QK], a["L0_conv_wq"]), (w_in[:, QK:2 * QK], a["L0_conv_wk"]),
                    (w_in[:, 2 * QK:], a["L0_conv_wv"]), (denom[:], a["c_denom"]),
                    (n1w[:], a["L0_conv_norm1_w"].rearrange("(c o) -> c o", o=1)),
                    (n1b[:], a["L0_conv_norm1_b"].rearrange("(c o) -> c o", o=1)))
            for d, s in wsrc:
                sp.dma_start(d, s).then_inc(w_loaded, 16)
            sp.wait_ge(ready, 1)
            for h in range(HEADS):
                sp.dma_start(wp[h * VW:h * VW + DV, :], a["L0_conv_wproj"][h * DV:(h + 1) * DV, :]).then_inc(w_loaded, 16)

            def step(t, m, has):
                n = (m + 2) % U
                if has(t + 2):
                    after(sp, qk_lo, 1, t + 2, 1)
                    sp.nop().then_inc(e.passed, 1)
                    after(sp, t_mm, 4, t - 1)
                    for row, part in enumerate((0, 0, 0, 1, 1, 2)):
                        sp.dma_start(qs[row * DQ:(row + 1) * DQ, n],
                                     parts[0:QK, n % 2, part, :]).then_inc(stacked[n], 16)
                    for row, part in enumerate((0, 1, 2, 0, 1, 0)):
                        sp.dma_start(ks[row * DQ:(row + 1) * DQ, n],
                                     parts[QK:2 * QK, n % 2, part, :]).then_inc(stacked[n], 16)
            pipeline(sp, NP, U, 2, 0, step)

        NST = 6 * 2 * 16

        @block.tensor
        def _(pe):
            pe.wait_ge(w_done, 1)
            nc.tensor.matmul(psM[C:C + 1, 0:2 * QK + C], n1b[:], w_in[:], start=True, stop=True).then_inc(w_bias, 1)
            pe.wait_ge(w_done, 6)

            def s_unit(t, m, u):
                b, nt, hp = u // 4, u // 2 % 2, u % 2
                after(pe, s_max, 8, t, u - 1)
                for h in (2 * hp, 2 * hp + 1):
                    mm = nc.tensor.matmul(psS[:, u % 2, (h % 2) * TOK:(h % 2 + 1) * TOK],
                                          qs[0:KQ, m, h, b * TOK + nt * P:b * TOK + nt * P + P],
                                          ks[0:KQ, m, h, b * TOK:(b + 1) * TOK], start=True, stop=True)
                mm.then_inc(s_mm, 1)

            def t_unit(t, m, u):
                b, hp = u // 2, u % 2
                after(pe, t_exp, 4, t, u - 1)
                for h in (2 * hp, 2 * hp + 1):
                    for kt in range(2):
                        mm = nc.tensor.matmul(psT[:, u % 2, h % 2, kt * TOK:(kt + 1) * TOK],
                                              ks[0:KM, m, h, b * TOK + kt * P:b * TOK + kt * P + P],
                                              qs[0:KM, m, h, b * TOK:(b + 1) * TOK], start=True, stop=True)
                mm.then_inc(t_mm, 1)

            def pv(t, m, b):
                after(pe, t_exp, 4, t, 2 * b + 2)
                if b == 0:
                    after(pe, v_sb, 1, t, 1)
                    after(pe, d_ln, 1, t)
                for kt in range(2):
                    for h in range(HEADS):
                        mm = nc.tensor.matmul(psO[h * VW:(h + 1) * VW, b * TOK:(b + 1) * TOK],
                                              vs[:, m, b * 2 + kt, h * VW:(h + 1) * VW],
                                              pr[:, 2 * b + h // 2, h % 2, kt, :],
                                              start=(kt == 0), stop=(kt == 1), skip_group_check=True)
                mm.then_inc(pv_mm, 1)

            def step(t, m, has):
                n, l, o = (m + 2) % U, (m - 1) % U, (m - 2) % U
                if has(t - 1):
                    if has(t + 1):
                        after(pe, v_sb, 1, t + 1, 1)
                    if has(t - 3):
                        after(pe, p_sb, 1, t - 3, 1)
                    after(pe, nm2, 1, t - 1, 1)
                    nc.tensor.transpose(psM[0:2 * HEADS * B * 2, 0:P // 2].bitcast(BF16),
                                        nmx[:].rearrange("p a h g -> p (a h g)"), identb[:]).then_inc(nmt_mm, 1)
                if has(t):
                    pe.wait_ge(stacked[m], stack_count(t, m, U) * NST)
                    s_unit(t, m, 0)
                    s_unit(t, m, 1)
                if has(t + 2):
                    after(pe, staged, 1, t + 2, 1)
                    after(pe, nmt_sb, 1, t)
                    if isinstance(t, int) and t <= 0:
                        after(pe, v_sb, 1, t + 2)
                    nc.tensor.matmul(psM[:], wqk[:], xw[:, n % 2, :], start=True, stop=True).then_inc(qk_mm, 1)
                if has(t):
                    s_unit(t, m, 2)
                if has(t - 2):
                    pv(t - 2, o, 1)
                if has(t):
                    s_unit(t, m, 3)
                if has(t):
                    s_unit(t, m, 4)
                if has(t - 1):
                    pe.wait_ge(maxrow[l], stack_count(t - 1, l, U) * 16)
                    t_unit(t - 1, l, 0)
                if has(t - 2):
                    after(pe, o_sb, 1, t - 2, 1)
                    nc.tensor.matmul(psO[:], denom[:], os_[:], start=True, stop=True).then_inc(d_mm, 1)
                if has(t):
                    s_unit(t, m, 5)
                if has(t + 2):
                    after(pe, qk_hi, 1, t + 2, 1)
                    after(pe, qk_rest, 1, t + 2, 1)
                    for g in range(4):
                        mm = nc.tensor.matmul(psM[:, g * P:(g + 1) * P], xw[:, n % 2, g * P:(g + 1) * P],
                                              wv[:].rearrange("c h v -> c (h v)"), start=True, stop=True)
                    mm.then_inc(v_mm, 1)
                if has(t - 1):
                    t_unit(t - 1, l, 1)
                if has(t):
                    s_unit(t, m, 6)
                if has(t - 1):
                    t_unit(t - 1, l, 2)
                if has(t):
                    s_unit(t, m, 7)
                if has(t - 2):
                    after(pe, o_n, 1, t - 2, 1)
                    if has(t + 2):
                        after(pe, v_sb, 1, t + 2, 1)
                    else:
                        after(pe, nmt_sb, 1, min(t, NP))
                    nc.tensor.matmul(psM[0:C, :], wp[:], rcp[:], start=True, stop=True).then_inc(p_mm, 1)
                if has(t - 1):
                    pv(t - 1, l, 0)
                if has(t - 1):
                    t_unit(t - 1, l, 3)
            pipeline(pe, NP, U, 2, 2, step)

        @block.scalar
        def _(act):
            act.preload_act_table_set("natural_log_exp_and_others")

            def exp(t, u):
                after(act, t_mm, 4, t, u + 1)
                if u % 2 == 0:
                    after(act, pv_mm, 2, t, u // 2 - 1)
                nc.scalar.activation(pr[:, u].rearrange("p h k n -> p h (k n)"), psT[:, u % 2, :, :],
                                     ACT.Exp).then_inc(t_exp, 1)

            def step(t, m, has):
                n, l = (m + 2) % U, (m - 1) % U
                if has(t - 1):
                    after(act, nmt_sb, 1, t - 1, 1)
                    nc.scalar.dma_start(qs[KQ:KM, l, :, :], nmt[:, :]).then_inc(maxrow[l], 16)
                if has(t + 2):
                    after(act, qk_mm, 1, t + 2, 1)
                    if has(t):
                        act.wait_ge(stacked[m], stack_count(t, m, U) * NST)
                    nc.scalar.copy(parts[:, n % 2, 0, :], psM[:]).then_inc(qk_hi, 1)
                if has(t - 2):
                    after(act, pv_mm, 2, t - 2, 2)
                    after(act, o_n, 1, t - 2)
                    nc.scalar.copy(os_[:], psO[:]).then_inc(o_sb, 1)
                if has(t + 2):
                    after(act, qk_rest, 1, t + 2, 1)
                    nc.scalar.copy(parts[:, n % 2, 1, :], rest[:]).then_inc(qk_mid, 1)
                if has(t - 1):
                    exp(t - 1, 0)
                if has(t - 2):
                    after(act, d_mm, 1, t - 2, 1)
                    after(act, p_mm, 1, t - 2)
                    nc.scalar.activation(rcp[:], psO[:], ACT.Ln).then_inc(d_ln, 1)
                    after(act, d_ln, 1, t - 2, 1)
                    nc.scalar.activation(rcp[:], rcp[:], ACT.Exp, scale=-1.0).then_inc(d_rcp, 1)
                if has(t - 1):
                    exp(t - 1, 1)
                    exp(t - 1, 2)
                if has(t - 2):
                    after(act, p_mm, 1, t - 2, 1)
                    after(act, acc, 2, t - 2)
                    nc.scalar.copy(pw[:], psM[0:C, :]).then_inc(p_sb, 1)
                if has(t - 1):
                    exp(t - 1, 3)
            pipeline(act, NP, U, 2, 2, step)

        @block.vector
        def _(dve):
            def by_head(x):
                return x.rearrange("c (h d) -> c h d", h=HEADS)

            def by_channel(x):
                return x.rearrange("c (d h) -> c h d", h=HEADS)

            nc.vector.memset(wp[:], 0.0).then_inc(ready, 1)
            nc.vector.memset(ys[C:C + 1], 1.0).then_inc(ready, 1)
            nc.vector.memset(ks[KQ:KM], 1.0).then_inc(ready, 1)
            nc.vector.memset(half[:], 0.5).then_inc(ready, 1)
            nc.vector.memset(wv[:], 0.0).then_inc(ready, 1)
            nc.vector.tensor_copy(identb[:], e.ident[:]).then_inc(ready, 1)
            dve.wait_ge(w_loaded, 16 * (6 + HEADS))
            dve.nop().then_inc(w_done, 1)
            dve.wait_ge(ready, 6)
            nc.vector.tensor_scalar(by_channel(wqk[0:C, 0:QK]), by_head(w_in[:, 0:QK]), n1w[:], DQ ** -0.5,
                                    ALU.mult, ALU.mult).then_inc(w_done, 1)
            nc.vector.tensor_scalar(by_channel(wqk[0:C, QK:]), by_head(w_in[:, QK:2 * QK]), n1w[:], None,
                                    ALU.mult).then_inc(w_done, 1)
            nc.vector.tensor_scalar(wv[0:C, :, 0:DV], w_in[:, 2 * QK:].rearrange("c (h v) -> c h v", h=HEADS),
                                    n1w[:], None, ALU.mult).then_inc(w_done, 1)
            dve.wait_ge(w_bias, 1)
            nc.vector.tensor_scalar(by_channel(wqk[C:C + 1, 0:QK]), by_head(psM[C:C + 1, 0:QK]), DQ ** -0.5, None, ALU.mult).then_inc(ready, 1)
            nc.vector.tensor_copy(by_channel(wqk[C:C + 1, QK:]), by_head(psM[C:C + 1, QK:2 * QK])).then_inc(ready, 1)
            nc.vector.tensor_copy(wv[C:C + 1, :, 0:DV],
                                  psM[C:C + 1, 2 * QK:2 * QK + C].rearrange("c (h v) -> c h v", h=HEADS)).then_inc(w_done, 1)
            nc.vector.memset(wv[C:C + 1, :, DV:DV + 1], 1.0).then_inc(w_done, 1)

            def reduce(t, u):
                b, nt, hp = u // 4, u // 2 % 2, u % 2
                after(dve, s_mm, 8, t, u + 1)
                if u == 0:
                    after(dve, nm2, 1, t)
                nc.vector.tensor_reduce(mx[:, 2 * hp:2 * hp + 2, b * 2 + nt], psS[:, u % 2, :].rearrange("p (h k) -> p h k", h=2),
                                        AX.X, ALU.max).then_inc(s_max, 1)

            def step(t, m, has):
                n = (m + 2) % U
                if has(t - 1):
                    after(dve, nmt_mm, 1, t - 1, 1)
                    if has(t - 2):
                        dve.wait_ge(maxrow[(m - 2) % U], stack_count(t - 2, (m - 2) % U, U) * 16)
                    nc.vector.tensor_copy(nmt[:], psM[0:2 * HEADS * B * 2, 0:P // 2].bitcast(BF16)).then_inc(nmt_sb, 1)
                if has(t):
                    reduce(t, 0)
                if has(t):
                    reduce(t, 1)
                    reduce(t, 2)
                if has(t + 2):
                    after(dve, qk_hi, 1, t + 2, 1)
                    after(dve, qk_lo, 1, t + 2)
                    nc.vector.tensor_tensor(rest[:], psM[:], parts[:, n % 2, 0, :], ALU.subtract).then_inc(qk_rest, 1)
                if has(t):
                    for u in range(3, 6):
                        reduce(t, u)
                if has(t + 2):
                    after(dve, v_mm, 1, t + 2, 1)
                    after(dve, pv_mm, 2, t - 1)
                    nc.vector.tensor_copy(vs[:, n].rearrange("p g v -> p (g v)"), psM[:]).then_inc(v_sb, 1)
                if has(t - 2):
                    after(dve, d_rcp, 1, t - 2, 1)
                    nc.vector.tensor_tensor(rcp[:], os_[:], rcp[:], ALU.mult).then_inc(o_n, 1)
                if has(t):
                    reduce(t, 6)
                    reduce(t, 7)
                    after(dve, s_max, 8, t, 8)
                    after(dve, nmt_mm, 1, t)
                    nc.vector.tensor_scalar(nmx[:, 0], mx[:], -1.0, None, ALU.mult).then_inc(nm1, 1)
                    after(dve, nm1, 1, t, 1)
                    nc.vector.scalar_tensor_tensor(out=nmx[:, 1], in0=mx[:], scalar=-1.0, in1=nmx[:, 0],
                                                   op0=ALU.mult, op1=ALU.subtract).then_inc(nm2, 1)
            pipeline(dve, NP, U, 2, 2, step)

        @block.gpsimd
        def _(pool):
            FIN = 5
            LAG = 5

            def fixed(v):
                return isinstance(v, int)

            def one(buffers, n):
                return buffers[:, n] if fixed(n) else buffers[:, bass.ds(n, 1)].squeeze(1)

            def row0(i):
                return LAST if fixed(i) and i == NSTRIP - 1 else i * STEP

            def load(i):
                pool.dma_start(one(ys[0:C], i % 2).rearrange("c b r w -> c b (r w)"),
                               y4[:, :, bass.ds(row0(i) * W, SC)]).then_inc(y_in, 16)

            def stage(i, j):
                p = i * NW + j
                after(pool, v_mm, 1, p, -1)
                col = LAST if fixed(j) and j == NW - 1 else j * STEP
                for b in range(B):
                    last = nc.gpsimd.tensor_copy(
                        one(xw, p % 2)[:, b * TOK:(b + 1) * TOK].rearrange("c (r w) -> c r w", r=PS),
                        one(ys, i % 2)[:, b, :, bass.ds(col, PS)])
                last.then_inc(staged, 1)

            def split(p):
                part = one(parts, p % 2)
                after(pool, qk_mid, 1, p, 1)
                nc.gpsimd.tensor_tensor(part[:, 2, :], rest[:], part[:, 1, :], ALU.subtract).then_inc(qk_lo, 1)

            def gather(i, j):
                p = i * NW + j
                opening, closing = fixed(j) and j == 0, fixed(j) and j == NW - 1
                after(pool, p_sb, 1, p, 1)
                after(pool, acc, 2, p)
                if opening and not (fixed(i) and i < 2):
                    after(pool, a_out, 16, i, -16)
                    after(pool, fin, FIN, i, -1)
                seen = 0 if opening else PS - 2 if closing else PS - STEP
                col = LAST if closing else j * STEP
                strip_ = one(av, i % 2)
                o3 = pw[:].rearrange("c (r w) -> c r w", w=PS)
                pool.nop().then_inc(e.passed, 1)
                if seen:
                    both = strip_[:, :, bass.ds(col, seen)]
                    nc.gpsimd.tensor_tensor(both, both, o3[:, :, 0:seen], ALU.add).then_inc(acc, 1)
                    nc.gpsimd.tensor_copy(strip_[:, :, bass.ds(col + seen, PS - seen)], o3[:, :, seen:]).then_inc(acc, 1)
                else:
                    nc.gpsimd.tensor_copy(strip_[:, :, 0:PS], o3).then_inc(acc, 2)

            def halve(i, first, last):
                two = one(av, i % 2)[:, :, STEP * (first + 1):STEP * (last + 1)].rearrange("c r (k s) -> c r k s", s=STEP)[:, :, :, 0:2]
                nc.gpsimd.tensor_tensor(two, two, half[:].unsqueeze(1).unsqueeze(1).to_broadcast([C, B * PS, last - first, 2]),
                                        ALU.mult).then_inc(fin, 1)

            def finish(i, part):
                mine, theirs = one(av, i % 2), one(av, (i + 1) % 2)
                final, top_strip = fixed(i) and i == NSTRIP - 1, fixed(i) and i == 0
                n = PS - 2 if final else 2
                if part == 0:
                    after(pool, acc, 2 * NW, i, 2 * (NW - LAG + 2))
                    after(pool, fin, FIN, i)
                    pool.nop().then_inc(e.passed, 1)
                    halve(i, 0, NW - LAG)
                if part == 1:
                    after(pool, acc, 2 * NW, i, 2 * NW)
                    after(pool, fin, FIN, i, 1)
                    pool.nop().then_inc(e.passed, 1)
                    halve(i, NW - LAG, NW - 2)
                    dup = mine[:, :, LAST:LAST + PS - 2]
                    nc.gpsimd.tensor_tensor(dup, dup, half[:].unsqueeze(1).to_broadcast([C, B * PS, PS - 2]),
                                            ALU.mult).then_inc(fin, 1)
                    after(pool, fin, FIN, i, 3)
                    pool.nop().then_inc(e.passed, 1)
                    if top_strip:
                        pool.nop().then_inc(fin, 1)
                    else:
                        for b in range(B):
                            top = mine[:, b * PS:b * PS + n, :]
                            last = nc.gpsimd.tensor_tensor(top, top, theirs[:, (b + 1) * PS - n:(b + 1) * PS, :], ALU.add)
                        last.then_inc(fin, 1)
                if part == 2:
                    after(pool, fin, FIN, i, 4)
                    pool.nop().then_inc(e.passed, 1)
                    if top_strip:
                        pool.nop().then_inc(fin, 1)
                    else:
                        for b in range(B):
                            for r in range(0, n, 2):
                                top = mine[:, b * PS + r:b * PS + r + 2, :]
                                last = nc.gpsimd.tensor_tensor(top, top, half[:].unsqueeze(1).to_broadcast([C, 2, W]), ALU.mult)
                        last.then_inc(fin, 1)
                    rows = PS if final else 2 if fixed(i) and i == NSTRIP - 2 else STEP
                    after(pool, fin, FIN, i, FIN)
                    pool.dma_start(a4[:, :, bass.ds(row0(i) * W, rows * W)],
                                   mine.rearrange("c (b r) w -> c b (r w)", b=B)[:, :, 0:rows * W]).then_inc(a_out, 16)

            def slot(i, j):
                p = i * NW + j
                if not fixed(p) or 1 <= p <= NP:
                    split(p - 1)
                if not fixed(p) or p < NP:
                    stage(i, j)
                if not fixed(p) or p >= LAG:
                    if fixed(j) and j < LAG:
                        gather(i - 1, NW - LAG + j)
                    else:
                        gather(i, j - LAG)

            def strip(i):
                follows = not fixed(i) or i > 0
                pool.wait_ge(y_in, i * 16 + 16)
                for j in range(LAG):
                    slot(i, j)
                    if j == 1 and follows:
                        finish(i - 1, 0)
                if follows:
                    finish(i - 1, 1)
                slot(i, LAG)
                if follows:
                    finish(i - 1, 2)
                slot(i, LAG + 1)
                if not fixed(i) or i < NSTRIP - 1:
                    after(pool, staged, NW, i)
                    load(i + 1)
                with pool.Fori(LAG + 2, NW - 1) as j:
                    slot(i, j)
                slot(i, NW - 1)

            pool.wait_ge(ready, 8)
            load(0)
            strip(0)
            strip(1)
            with pool.Fori(2, NSTRIP - 2) as i:
                strip(i)
            strip(NSTRIP - 2)
            strip(NSTRIP - 1)
            for j in range(LAG):
                slot(NSTRIP, j)
            for part in range(3):
                finish(NSTRIP - 1, part)
            pool.wait_ge(a_out, 16 * NSTRIP)


def stage_expand(nc, e):
    U = 2
    NT = 4
    N = NT * T
    CH = HW // N
    RW = N // W
    G = MLP // C
    with ExitStack() as ctx:
        def sb(name, shape, dt=F32):
            return ctx.enter_context(nc.sbuf_tensor(f"ex_{name}", shape, dt))

        def sem(name):
            return ctx.enter_context(nc.semaphore(f"ex_{name}"))

        xin, ain, tin = (sb(n, [C, U, N]) for n in ("xin", "ain", "tin"))
        yt = sb("yt", [C, U, N])
        sq, rstd = sb("sq", [C, NT, T]), sb("rstd", [C, NT, T])
        hid = sb("hid", [C, U, G, RW, WP])
        w1 = sb("w1", [C, MLP])
        w1n = sb("w1n", [C, MLP])
        vecs = sb("vecs", [C, 4])
        bias = sb("bias", [C, G])
        bc = sb("bc", [C, B])
        pc = ctx.enter_context(nc.psum_tensor("ex_pc", [C, NT, T], F32))
        pv = ctx.enter_context(nc.psum_tensor("ex_pv", [C, 2, T], F32))
        ph = ctx.enter_context(nc.psum_tensor("ex_ph", [C, 2, T], F32))
        w_in, prep, prep_mm = sem("w_in"), sem("prep"), sem("prep_mm")
        loaded = [sem(f"loaded{m}") for m in range(U)]
        stored = [sem(f"stored{m}") for m in range(U)]
        summed, centred, squared, varied, logged, inverted, normed, h_mm, h_act = (
            sem(n) for n in ("summed", "centred", "squared", "varied", "logged", "inverted", "normed", "h_mm", "h_act"))
        a = e.aps
        hid4 = e.hid.rearrange("(g c) b (k r) w -> c g (b k) (r w)", g=G, r=RW)
        block = ctx.enter_context(nc.Block())

        @block.sync
        def _(sp):
            for d, s in ((w1[:], a["L0_conv_fc1_w"]), (vecs[:, 0:1], column(a["L0_conv_norm2_w"])),
                         (vecs[:, 1:2], column(a["L0_conv_norm2_b"])), (vecs[:, 2:3], column(a["L0_conv_fc1_b"][0:C])),
                         (vecs[:, 3:4], column(a["L0_conv_fc1_b"][C:MLP]))):
                sp.dma_start(d, s).then_inc(w_in, 16)
            for b in range(B):
                g0 = b * CH

                def step(t, m, has):
                    g = t + g0
                    if has(t + 2):
                        after(sp, summed, NT, g + 1)
                        cols = bass.ds((t + 2) * N, N)
                        sp.dma_start(xin[:, m, :], e.x[b][:, cols]).then_inc(loaded[m], 16)
                        sp.dma_start(ain[:, m, :], e.attn[b][:, cols]).then_inc(loaded[m], 16)
                    if has(t - 1):
                        o = (m - 1) % U
                        after(sp, h_act, 2 * NT, g)
                        sp.dma_start(hid4[:, :, bass.ds(g - 1, 1), :],
                                     hid[:, o].rearrange("c g (k r) w -> c g k (r w)", k=1)).then_inc(stored[o], 16)
                pipeline(sp, CH, U, 2, 1, step)
            for m in range(U):
                sp.wait_ge(stored[m], 16 * (B * CH // U))

        @block.tensor
        def _(pe):
            pe.wait_ge(prep, 2)
            for b in range(B):
                nc.tensor.matmul(pv[:, 0, b:b + 1], e.centre[:], e.shift0[:, b:b + 1], start=True, stop=True)
            for k in range(G):
                mm = nc.tensor.matmul(pv[:, 0, B + k:B + k + 1], w1[:, k * C:(k + 1) * C], vecs[:, 1:2], start=True, stop=True)
            mm.then_inc(prep_mm, 1)
            pe.wait_ge(prep, 4)
            for b in range(B):
                g0 = b * CH

                def step(t, m, has):
                    g = t + g0
                    n, o = (m + 1) % U, (m - 1) % U
                    if has(t):
                        for s in range(NT):
                            after(pe, squared, NT, g, s + 1)
                            after(pe, logged, NT, g, s - 1)
                            nc.tensor.matmul(pv[:, s % 2, :], e.mean[:], sq[:, s, :], start=True, stop=True).then_inc(varied, 1)
                    for k in range(2 * NT):
                        if has(t - 1):
                            s = k // 2
                            after(pe, normed, NT, g - 1, s + 1)
                            after(pe, h_act, 2 * NT, g - 1, max(k - 1, 0))
                            nc.tensor.matmul(ph[:, k % 2, :], w1n[:, k % 2 * C:(k % 2 + 1) * C],
                                             yt[:, o, s * T:(s + 1) * T], start=True, stop=True).then_inc(h_mm, 1)
                        if k % 2 and has(t + 1):
                            s = k // 2
                            after(pe, summed, NT, g + 1, s + 1)
                            after(pe, normed, NT, g, s + 1)
                            nc.tensor.matmul(pc[:, s, :], e.centre[:], tin[:, n, s * T:(s + 1) * T],
                                             start=True, stop=True).then_inc(centred, 1)
                pipeline(pe, CH, U, 1, 1, step)

        @block.scalar
        def _(act):
            act.wait_ge(prep, 4)
            for b in range(B):
                g0 = b * CH

                def step(t, m, has):
                    g = t + g0
                    o = (m - 1) % U
                    if has(t):
                        act.preload_act_table_set("natural_log_exp_and_others")
                        for s in range(NT):
                            after(act, varied, NT, g, s + 1)
                            after(act, normed, NT, g - 1, s + 1)
                            nc.scalar.activation(rstd[:, s, :], pv[:, s % 2, :], ACT.Ln, bias=e.eps[0:C, :]).then_inc(logged, 1)
                            after(act, logged, NT, g, s + 1)
                            nc.scalar.activation(rstd[:, s, :], rstd[:, s, :], ACT.Exp, scale=-0.5).then_inc(inverted, 1)
                    if has(t - 1):
                        act.preload_act_table_set("gelu_and_others")
                        if has(t - 3) or g0:
                            act.wait_ge(stored[o], 16 * stack_count(g - 3, o, U))
                    for k in range(2 * NT):
                        if has(t - 1):
                            s = k // 2
                            after(act, h_mm, 2 * NT, g - 1, k + 1)
                            rows = T // W
                            nc.scalar.activation(hid[:, o, k % 2, s * rows:(s + 1) * rows, PAD:PAD + W],
                                                 ph[:, k % 2, :].rearrange("c (r w) -> c r w", w=W), ACT.Gelu,
                                                 bias=bias[:, k % 2:k % 2 + 1]).then_inc(h_act, 1)
                        if k % 2 and has(t + 1):
                            s = k // 2
                            after(act, centred, NT, g + 1, s + 1)
                            after(act, varied, NT, g, s + 1)
                            nc.scalar.activation(sq[:, s, :], pc[:, s, :], ACT.Square,
                                                 bias=bc[:, b:b + 1]).then_inc(squared, 1)
                pipeline(act, CH, U, 1, 3, step)

        @block.vector
        def _(dve):
            nc.vector.memset(hid[:], 0.0).then_inc(prep, 1)
            dve.wait_ge(w_in, 16 * 5)
            nc.vector.tensor_scalar(w1n[:], w1[:], vecs[:, 0:1], None, ALU.mult).then_inc(prep, 1)
            dve.wait_ge(prep_mm, 1)
            nc.vector.tensor_copy(bc[:], pv[:, 0, 0:B]).then_inc(prep, 1)
            nc.vector.tensor_tensor(bias[:], pv[:, 0, B:B + G], vecs[:, 2:4], ALU.add).then_inc(prep, 1)
            dve.wait_ge(prep, 4)
            for b in range(B):
                g0 = b * CH

                def step(t, m, has):
                    g = t + g0
                    n = (m + 1) % U
                    if has(t + 1):
                        dve.wait_ge(loaded[n], 32 * stack_count(g + 1, n, U))
                        after(dve, centred, NT, g)
                        for s in range(NT):
                            sl = slice(s * T, (s + 1) * T)
                            nc.vector.scalar_tensor_tensor(
                                out=tin[:, n, sl], in0=xin[:, n, sl], scalar=e.gain0[:, b:b + 1], in1=ain[:, n, sl],
                                op0=ALU.mult, op1=ALU.add).then_inc(summed, 1)
                    if has(t):
                        for s in range(NT):
                            after(dve, inverted, NT, g, s + 1)
                            if s == 0:
                                after(dve, h_mm, 2 * NT, g - 1)
                            nc.vector.scalar_tensor_tensor(
                                out=yt[:, m, s * T:(s + 1) * T], in0=pc[:, s, :], scalar=bc[:, b:b + 1],
                                in1=rstd[:, s, :], op0=ALU.add, op1=ALU.mult).then_inc(normed, 1)
                pipeline(dve, CH, U, 1, 0, step)


def stage_conv(nc, e):
    U = 3
    G = MLP // C
    HALF = H // P
    NH = 2 * KS
    HM = 32
    F = P - 1
    with ExitStack() as ctx:
        def sb(name, shape, dt=F32):
            return ctx.enter_context(nc.sbuf_tensor(f"cv_{name}", shape, dt))

        def sem(name):
            return ctx.enter_context(nc.semaphore(f"cv_{name}"))

        taps = sb("taps", [C, G, KS * KS])
        tabs = sb("tabs", [C, G, KS, TAB])
        bias = sb("bias", [P, MLP])
        t_in, t_set, t_out = sem("t_in"), sem("t_set"), sem("t_out")
        with nc.Block() as block:
            @block.sync
            def _(sp):
                sp.dma_start(taps[:], e.aps["L0_conv_dw_w"].rearrange("(g c) o i j -> c g (o i j)", g=G)).then_inc(t_in, 16)
                sp.dma_start(bias[:], e.aps["L0_conv_dw_b"].rearrange("(o n) -> o n", o=1).to_broadcast([P, MLP])).then_inc(t_in, 16)
                sp.wait_ge(t_set, 1 + G)
                sp.dma_start(e.tab.rearrange("(g c) k n -> c g (k n)", g=G), tabs[:].rearrange("c g k n -> c g (k n)")).then_inc(t_out, 16)
                sp.wait_ge(t_out, 16)
                sp.wait_ge(t_in, 32)

            @block.vector
            def _(dve):
                nc.vector.memset(tabs[:], 0.0).then_inc(t_set, 1)
                dve.wait_ge(t_set, 1)
                dve.wait_ge(t_in, 32)
                for g in range(G):
                    nc.vector.tensor_copy(tabs[:, g, :, F:F + KS],
                                          taps[:, g].rearrange("c (i j) -> c j i", j=KS)).then_inc(t_set, 1)

        hin = sb("hin", [P, U, B, HALF, WP])
        halo = sb("halo", [NH, U, HALF, B, W])
        bandr = sb("bandr", [P, U, KS, P])
        band = sb("band", [P, U, KS, P])
        hbandr = sb("hbandr", [NH, U, HALF, HM])
        hband = sb("hband", [NH, U, HALF, HM])
        d = sb("d", [P, U, HALF, T])
        z = sb("z", [P, U, B, HALF, W])
        ps = ctx.enter_context(nc.psum_tensor("cv_ps", [P, U, HALF, T], F32))
        loaded = [sem(f"loaded{m}") for m in range(U)]
        stored = [sem(f"stored{m}") for m in range(U)]
        turned, c_mm, c_act, added = sem("turned"), sem("c_mm"), sem("c_act"), sem("added")
        hidt, tabt = e.hid.tensor, e.tab.tensor
        NL = (2 + HALF * B + HALF) * 16
        z4 = e.z.rearrange("m b (g r w) -> m r (b g) w", g=HALF, r=P)
        hid4 = e.hid.rearrange("m b (g r) w -> m r (b g) w", g=HALF)
        block = ctx.enter_context(nc.Block())

        @block.sync
        def _(sp):
            def step(t, m, has):
                if has(t + U):
                    c = t + U
                    after(sp, added, HALF, t, HALF)
                    sp.dma_start(hin[:, m].rearrange("p b g w -> p (b g) w"), hid4[bass.ds(c, 1)].squeeze(0)).then_inc(loaded[m], 16)
                    sp.dma_start(bandr[:, m], bass.AP(tabt, c * (KS * TAB) + 2, [[1, P], [TAB, KS], [1, P]])).then_inc(loaded[m], 16)
                    for g, row in ((0, P), (1, P - 2)):
                        for b in range(B):
                            sp.dma_start(halo[:, m, g, b], bass.AP(hidt, c * (B * H * WP) + (b * H + row) * WP,
                                                                   [[1, KS], [WP, 2], [1, W]])).then_inc(loaded[m], 16)
                    for g, first in ((0, P + 2), (1, P - HM)):
                        sp.dma_start(hbandr[:, m, g], bass.AP(tabt, c * (KS * TAB) + first,
                                                              [[TAB, KS], [1, 2], [1, HM]])).then_inc(loaded[m], 16)
                if has(t - 1):
                    o = (m - 1) % U
                    after(sp, added, HALF, t)
                    sp.dma_start(z4[bass.ds(t - 1, 1)].squeeze(0), z[:, o].rearrange("p b g w -> p (b g) w")).then_inc(stored[o], 16)
            pipeline(sp, MLP, U, U, 1, step)
            for m in range(U):
                sp.wait_ge(stored[m], 16 * (MLP // U))

        @block.gpsimd
        def _(pool):
            def step(t, m, has):
                pool.wait_ge(loaded[m], NL * stack_count(t, m, U))
                after(pool, c_mm, HALF, t - 1)
                pool.nop().then_inc(e.passed, 1)
                nc.gpsimd.tensor_copy(band[:, m], bandr[:, m, :, P - 1::-1]).then_inc(turned, 1)
                nc.gpsimd.tensor_copy(hband[:, m], hbandr[:, m, :, HM - 1::-1]).then_inc(turned, 1)
            pipeline(pool, MLP, U, 0, 0, step)

        @block.tensor
        def _(pe):
            def step(t, m, has):
                pe.wait_ge(loaded[m], NL * stack_count(t, m, U))
                after(pe, turned, 2, t, 2)
                after(pe, c_act, HALF, t - 1)
                def taps_of(g, dx):
                    return nc.tensor.matmul(ps[:, m, g, :], band[:, m, dx, :], hin[:, m, :, g, dx:dx + W],
                                            start=(dx == 0), stop=(dx == KS - 1))
                for g in range(HALF):
                    for dx in range(KS - 1):
                        taps_of(g, dx)
                for g in range(HALF):
                    rows = slice(P - HM, P) if g == 0 else slice(0, HM)
                    nc.tensor.matmul(ps[rows, m, g, :], hband[:, m, g, :], halo[:, m, g, :, :],
                                     start=False, stop=False, skip_group_check=True)
                for g in range(HALF):
                    taps_of(g, KS - 1).then_inc(c_mm, 1)
            pipeline(pe, MLP, U, 0, 0, step)

        @block.scalar
        def _(act):
            act.preload_act_table_set("gelu_and_others")

            def step(t, m, has):
                after(act, added, HALF, t - 1)
                for g in range(HALF):
                    after(act, c_mm, HALF, t, g + 1)
                    act.nop().then_inc(e.passed, 1)
                    bias_c = bias[:, t:t + 1] if isinstance(t, int) else bias[:, bass.ds(t, 1)]
                    nc.scalar.activation(d[:, m, g, :], ps[:, m, g, :], ACT.Gelu, bias=bias_c).then_inc(c_act, 1)
            pipeline(act, MLP, U, 0, 0, step)

        @block.vector
        def _(dve):
            def step(t, m, has):
                if not has(t):
                    return
                if has(t - U):
                    dve.wait_ge(stored[m], 16 * stack_count(t - U, m, U))
                for g in range(HALF):
                    after(dve, c_act, HALF, t, g + 1)
                    nc.vector.tensor_tensor(z[:, m, :, g], d[:, m, g].rearrange("p (b w) -> p b w", b=B),
                                            hin[:, m, :, g, PAD:PAD + W], ALU.add).then_inc(added, 1)
            pipeline(dve, MLP, U, 0, U, step)


def stage_contract(nc, e):
    U = 4
    NT = 4
    N = NT * T
    CH = HW // N
    G = MLP // C
    with ExitStack() as ctx:
        def sb(name, shape, dt=F32):
            return ctx.enter_context(nc.sbuf_tensor(f"ct_{name}", shape, dt))

        def sem(name):
            return ctx.enter_context(nc.semaphore(f"ct_{name}"))

        zin = sb("zin", [C, U, G, N])
        xin, ain, res, out = (sb(n, [C, U, N]) for n in ("xin", "ain", "res", "out"))
        w2 = sb("w2", [C, G, C])
        b2 = sb("b2", [C, 1])
        gain, shift = sb("gain", [C, B]), sb("shift", [C, B])
        ps = ctx.enter_context(nc.psum_tensor("ct_ps", [C, NT, T], F32))
        w_in, prep = sem("w_in"), sem("prep")
        loaded = [sem(f"loaded{m}") for m in range(U)]
        stored = [sem(f"stored{m}") for m in range(U)]
        scaled, joined, f_mm, done, counted = (sem(n) for n in ("scaled", "joined", "f_mm", "done", "counted"))
        z4 = e.z.rearrange("(g c) b n -> b c g n", g=G)
        block = ctx.enter_context(nc.Block())

        @block.sync
        def _(sp):
            sp.dma_start(w2[:], e.aps["L0_conv_fc2_w"].rearrange("(g c) n -> c g n", g=G)).then_inc(w_in, 16)
            sp.dma_start(b2[:], column(e.aps["L0_conv_fc2_b"])).then_inc(w_in, 16)
            for b in range(B):
                g0 = b * CH

                def step(t, m, has):
                    g = t + g0
                    if has(t + U):
                        after(sp, done, NT, g + 1)
                        cols = bass.ds((t + U) * N, N)
                        sp.dma_start(zin[:, m], z4[b][:, :, cols]).then_inc(loaded[m], 16)
                        sp.dma_start(xin[:, m], e.x[b][:, cols]).then_inc(loaded[m], 16)
                        sp.dma_start(ain[:, m], e.attn[b][:, cols]).then_inc(loaded[m], 16)
                    if has(t - 1):
                        o = (m - 1) % U
                        after(sp, done, NT, g)
                        sp.dma_start(e.x1[b][:, bass.ds((t - 1) * N, N)], out[:, o]).then_inc(stored[o], 16)
                pipeline(sp, CH, U, U, 1, step)
            for m in range(U):
                sp.wait_ge(stored[m], 16 * (B * CH // U))

        @block.tensor
        def _(pe):
            pe.wait_ge(w_in, 32)
            for b in range(B):
                g0 = b * CH

                def step(t, m, has):
                    g = t + g0
                    pe.wait_ge(loaded[m], 48 * stack_count(g, m, U))
                    for s in range(NT):
                        after(pe, done, NT, g - 1, s + 1)
                        for k in range(G):
                            mm = nc.tensor.matmul(ps[:, s, :], w2[:, k, :], zin[:, m, k, s * T:(s + 1) * T],
                                                  start=(k == 0), stop=(k == G - 1))
                        mm.then_inc(f_mm, 1)
                pipeline(pe, CH, U, 0, 0, step)

        @block.scalar
        def _(act):
            act.wait_ge(prep, 2)
            for b in range(B):
                g0 = b * CH

                def step(t, m, has):
                    g = t + g0
                    act.wait_ge(loaded[m], 48 * stack_count(g, m, U))
                    after(act, done, NT, g - 1)
                    nc.scalar.activation(res[:, m], xin[:, m], ACT.Identity, bias=shift[:, b:b + 1],
                                         scale=gain[:, b:b + 1]).then_inc(scaled, 1)
                pipeline(act, CH, U, 0, 0, step)

        @block.gpsimd
        def _(pool):
            for b in range(B):
                g0 = b * CH

                def step(t, m, has):
                    g = t + g0
                    after(pool, scaled, 1, g, 1)
                    nc.gpsimd.tensor_tensor(res[:, m], res[:, m], ain[:, m], ALU.add).then_inc(joined, 1)
                pipeline(pool, CH, U, 0, 0, step)

        @block.vector
        def _(dve):
            nc.vector.tensor_scalar(gain[:], e.gain0[:], 1.0, None, ALU.add).then_inc(prep, 1)
            dve.wait_ge(w_in, 32)
            nc.vector.tensor_scalar(shift[:], e.shift0[:], b2[:], None, ALU.add).then_inc(prep, 1)
            for b in range(B):
                g0 = b * CH

                def step(t, m, has):
                    if not has(t):
                        return
                    g = t + g0
                    after(dve, joined, 1, g, 1)
                    if has(t - U) or g0:
                        dve.wait_ge(stored[m], 16 * stack_count(g - U, m, U))
                    for s in range(NT):
                        sl = slice(s * T, (s + 1) * T)
                        after(dve, f_mm, NT, g, s + 1)
                        nc.vector.tensor_tensor(out[:, m, sl], ps[:, s, :], res[:, m, sl], ALU.add).then_inc(done, 1)
                    for s in range(NT):
                        after(dve, done, NT, g, s + 1)
                        nc.vector.bn_stats(e.moments[:, bass.ds((g * NT + s) * 6, 6)],
                                           out[:, m, s * T:(s + 1) * T]).then_inc(counted, 1)
                pipeline(dve, CH, U, 0, U, step)


def stage_cluster(nc, e):
    U = 2
    N = BS * BS
    NB = (H // BS) * (W // BS)
    PR = W // BS
    Q = 4
    NQ = N // Q
    HM = H1 * NC1
    F = HD // P
    K1 = C + 1
    UN = 8
    HP = T // BS
    ZMAX, ZMIN = 17.33, -88.0
    TINY = 1e-24
    SC = 2.0 ** 20
    with ExitStack() as ctx:
        def sb(name, shape, dt=F32):
            return ctx.enter_context(nc.sbuf_tensor(f"cl_{name}", shape, dt))

        def sem(name):
            return ctx.enter_context(nc.semaphore(f"cl_{name}"))

        def pb(name, shape):
            return ctx.enter_context(nc.psum_tensor(f"cl_{name}", shape, F32))

        wfc, wvc = sb("wfc", [P, F, K1]), sb("wvc", [P, F, K1])
        wpo = sb("wpo", [C, HD])
        wft, wvt = sb("wft", [K1, HD]), sb("wvt", [K1, HD])
        wpt = sb("wpt", [P, F, C])
        bp = sb("bp", [C, 1])
        same = sb("same", [P, P])
        headc = sb("headc", [P, F, HM])
        first = sb("first", [P, 2 * Q * H1, NC1])
        alpha, beta = sb("alpha", [P, 1]), sb("beta", [P, 1])
        lnsc = sb("lnsc", [P, 1])
        onesb = sb("onesb", [P, 1], BF16)
        xs = sb("xs", [C, 2, BS, W])
        g = sb("g", [K1, U, N])
        fsq = sb("fsq", [P, U, F, N])
        fc, vc, vcb = (sb(n, [P, U, F, NC1]) for n in ("fc", "vc", "vcb"))
        fcs, n2c, rcn, cn = (sb(n, [P, F * NC1]) for n in ("fcs", "n2c", "rcn", "cn"))
        cnbd = sb("cnbd", [P, F, HM])
        dsb = sb("dsb", [K1, HM])
        gt = sb("gt", [P, U, Q * 2, K1])
        rn, cos = sb("rn", [P, NQ]), sb("cos", [P, NQ])
        z = sb("z", [P, U, NQ])
        sel, sel1, seln = (sb(n, [P, 2 * Q * H1]) for n in ("sel", "sel1", "seln"))
        best, lead = sb("best", [P, 2 * Q * H1]), sb("lead", [P, 2 * Q * H1])
        nwt, nwt2 = sb("nwt", [P, F * NC1]), sb("nwt2", [P, F * NC1])
        win = sb("win", [P, 2 * Q * H1, NC1])
        mask = sb("mask", [P, 2 * Q * H1, NC1], BF16)
        simm = sb("simm", [P, 2, P])
        simc = sb("simc", [P, NQ])
        agg = sb("agg", [HM, K1 + 1])
        cnt, rc = sb("cnt", [HM, 1]), sb("rc", [HM, 1])
        aggt = sb("aggt", [K1, HM])
        num = sb("num", [P, F, HM])
        gbd = sb("gbd", [P, Q, C])
        ps_p = pb("ps_p", [P, 2, T])
        ps_dn = pb("ps_dn", [P, 2, NQ])
        ps_st = pb("ps_st", [P, 2, NQ])
        ps_gt = pb("ps_gt", [P, 4, P])
        ps_o = pb("ps_o", [C, 2, T])
        ps_s = pb("ps_s", [P, T])
        w_in, prep, prep_mm, x_in, x_out = sem("w_in"), sem("prep"), sem("prep_mm"), sem("x_in"), [sem(f"x_out{m}") for m in range(2)]
        names = ("newton zs g_sb p_mm f_sq pooled c2_mm c2_max rcn_sb cn_sb cnbd_sb fcs_sb d_mm d_sb gt_mm gt_sb dn_mm n_max n_rn cos_sb "
                 "e_sb e1_sb sim_sb st_mm m1 won m5 simm_sb sc_mm sc_sb agg_mm agg_sb cnt_sb rc_sb at_mm at_sb av_mm nums "
                 "gg_mm gbd_sb o_mm o_done logged").split()
        S = {n: sem(n) for n in names}
        a = e.aps
        block = ctx.enter_context(nc.Block())

        @block.sync
        def _(sp):
            loads = ((wfc[:, :, 0:C], a["L1_conv_Wf"].rearrange("(f c) k -> c f k", f=F)),
                     (wvc[:, :, 0:C], a["L1_conv_Wv"].rearrange("(f c) k -> c f k", f=F)),
                     *((w[:, f, C:C + 1], column(a[name][f * P:(f + 1) * P])) for f in range(F)
                       for w, name in ((wfc, "L1_conv_bf"), (wvc, "L1_conv_bv"))),
                     (wpo[:], a["L1_conv_Wp"]), (bp[:], column(a["L1_conv_bp"])),
                     (same[:], a["c_same"]), (headc[:], a["c_headc"]), (first[:], a["c_first"]),
                     (alpha[:], a["L1_conv_sim_alpha"].rearrange("(o n) -> o n", o=1).to_broadcast([P, 1])),
                     (beta[:], a["L1_conv_sim_beta"].rearrange("(o n) -> o n", o=1).to_broadcast([P, 1])))
            for d, s in loads:
                sp.dma_start(d, s).then_inc(w_in, 16)
            for b in range(B):
                def step(t, m, has):
                    s = t + b * (H // BS)
                    if has(t + 1):
                        if has(t - 1) or b:
                            sp.wait_ge(x_out[(m + 1) % 2], 16 * stack_count(s - 1, (m + 1) % 2, 2))
                        after(sp, x_in, 16, s, 16)
                        sp.dma_start(xs[:, (m + 1) % 2].rearrange("c r w -> c (r w)"),
                                     e.x1[b][:, bass.ds((t + 1) * (BS * W), BS * W)]).then_inc(x_in, 16)
                    if has(t):
                        after(sp, S["o_done"], 2 * PR, s, 2 * PR)
                        sp.dma_start(e.out[b][:, bass.ds(t * (BS * W), BS * W)],
                                     xs[:, m].rearrange("c r w -> c (r w)")).then_inc(x_out[m], 16)
                pipeline(sp, H // BS, 2, 1, 1, step)
            for m in range(2):
                sp.wait_ge(x_out[m], 16 * B * (H // BS) // 2)

        def project(t, u):
            return (wft if u < 4 else wvt), u // 2 % 2, u % 2

        @block.tensor
        def _(pe):
            pe.wait_ge(w_in, 13 * 16)
            for w in (wfc, wvc):
                for f in range(F):
                    nc.tensor.transpose(ps_gt[0:K1, (w is wvc) * 2 + f, :], w[:, f, :], e.ident[:])
            for f in range(F):
                mm = nc.tensor.transpose(ps_s[:, f * C:(f + 1) * C], wpo[:, f * P:(f + 1) * P], e.ident[0:C, 0:C])
            mm.then_inc(prep_mm, 1)
            pe.wait_ge(prep, 7)
            for b in range(B):
                g0 = b * NB

                def unit(gi, m, u):
                    w, f, h = project(gi, u)
                    after(pe, S["pooled"], UN, gi, u - 1)
                    nc.tensor.matmul(ps_p[:, u % 2, :], w[:, f * P:(f + 1) * P], g[:, m, h * T:(h + 1) * T],
                                     start=True, stop=True).then_inc(S["p_mm"], 1)

                def turn(gi, m, r):
                    after(pe, S["gt_sb"], 2, gi, r)
                    for k in range(4):
                        mm = nc.tensor.transpose(ps_gt[:, k, 0:K1], g[:, m, (4 * r + k) * P:(4 * r + k + 1) * P],
                                                 e.ident[0:K1, 0:K1])
                    mm.then_inc(S["gt_mm"], 1)

                def step(t, m, has):
                    i = t + g0
                    A, Bk, Ck = has(t + 1), has(t), has(t - 1)
                    n = (m + 1) % U
                    if A:
                        after(pe, S["g_sb"], 1, i + 1, 1)
                        unit(i + 1, n, 0)
                    if Bk:
                        after(pe, S["gbd_sb"], 1, i - 1)
                        after(pe, S["fcs_sb"], 1, i, 1)
                        nc.tensor.matmul(ps_s[:, 0:F * NC1], same[:], fcs[:], start=True, stop=True).then_inc(S["c2_mm"], 1)
                    if Ck:
                        after(pe, S["zs"], 2, i - 1, 2)
                        after(pe, S["sc_sb"], 1, i - 1)
                        for k in range(2):
                            mm = nc.tensor.transpose(ps_st[:, 0, k * P:(k + 1) * P], z[:, n, k * P:(k + 1) * P], e.ident[:])
                        mm.then_inc(S["st_mm"], 1)
                    if A:
                        unit(i + 1, n, 1)
                    if Bk:
                        turn(i, m, 0)
                    if A:
                        unit(i + 1, n, 2)
                    if Bk:
                        after(pe, S["cos_sb"], 1, i)
                        for f in range(F):
                            for q in range(Q):
                                nc.tensor.matmul(ps_dn[q * HM:(q + 1) * HM, 0, :], headc[:, f, :], fsq[:, m, f, q * NQ:(q + 1) * NQ],
                                                 start=(f == 0), stop=(f == F - 1), skip_group_check=True)
                    if Bk:
                        after(pe, S["cnbd_sb"], 1, i, 1)
                        for f in range(F):
                            mm = nc.tensor.matmul(ps_s[0:K1, 0:HM], wfc[:, f, :], cnbd[:, f, :], start=(f == 0), stop=(f == F - 1))
                        mm.then_inc(S["d_mm"], 1)
                    if A:
                        unit(i + 1, n, 3)
                    if Bk:
                        after(pe, S["d_sb"], 1, i, 1)
                        for q in range(Q):
                            mm = nc.tensor.matmul(ps_dn[q * HM:(q + 1) * HM, 1, :], dsb[:], g[:, m, q * NQ:(q + 1) * NQ],
                                                  start=True, stop=True, skip_group_check=True)
                        mm.then_inc(S["dn_mm"], 1)
                        turn(i, m, 1)
                    if Ck:
                        after(pe, S["simm_sb"], 1, i - 1, 1)
                        for k in range(2):
                            mm = nc.tensor.transpose(ps_st[:, 1, k * P:(k + 1) * P], simm[:, k, :], e.ident[:])
                        mm.then_inc(S["sc_mm"], 1)
                        if Bk:
                            after(pe, S["d_sb"], 1, i, 1)
                        else:
                            after(pe, S["gbd_sb"], 1, i - 1)
                        after(pe, S["gt_sb"], 2, i - 1, 2)
                        for k in range(2 * Q):
                            nc.tensor.matmul(ps_s[0:HM, 0:K1], simm[:, k % 2, k // 2 * HM:(k // 2 + 1) * HM], gt[:, n, k, :],
                                             start=(k == 0), stop=(k == 2 * Q - 1))
                        mk = mask[:].rearrange("p (a h) m -> p a (h m)", a=2 * Q)
                        for k in range(2 * Q):
                            mm = nc.tensor.matmul(ps_s[0:HM, K1:K1 + 1], mk[:, (k % 2) * Q + k // 2, :], onesb[:],
                                                  start=(k == 0), stop=(k == 2 * Q - 1))
                        mm.then_inc(S["agg_mm"], 1)
                    if A:
                        unit(i + 1, n, 4)
                    if Ck:
                        after(pe, S["agg_sb"], 1, i - 1, 1)
                        pe.nop().then_inc(e.passed, 1)
                        nc.tensor.transpose(ps_s[0:K1, 0:HM], agg[:, 0:K1], e.ident[0:HM, 0:HM]).then_inc(S["at_mm"], 1)
                    if A:
                        unit(i + 1, n, 5)
                    if Ck:
                        after(pe, S["at_sb"], 1, i - 1, 1)
                        for f in range(F):
                            mm = nc.tensor.matmul(ps_s[:, f * HM:(f + 1) * HM], wvt[:, f * P:(f + 1) * P], aggt[:], start=True, stop=True)
                        mm.then_inc(S["av_mm"], 1)
                    if A:
                        unit(i + 1, n, 6)
                    if Ck:
                        after(pe, S["nums"], 2, i - 1, 2)
                        for f in range(F):
                            mm = nc.tensor.matmul(ps_s[0:HM, 0:C], num[:, f, :], wpt[:, f, :], start=(f == 0), stop=(f == F - 1))
                        mm.then_inc(S["gg_mm"], 1)
                    if A:
                        unit(i + 1, n, 7)
                    if Ck:
                        after(pe, S["gbd_sb"], 1, i - 1, 1)
                        after(pe, S["sc_sb"], 1, i - 1, 1)
                        for q in range(Q):
                            if q % 2 == 0:
                                after(pe, S["o_done"], 2, i - 1, q // 2 - 1)
                            mm = nc.tensor.matmul(ps_o[:, q // 2, q % 2 * NQ:(q % 2 + 1) * NQ], gbd[:, q, :], simc[:],
                                                  start=True, stop=True)
                            if q % 2:
                                mm.then_inc(S["o_mm"], 1)
                pipeline(pe, NB, U, 1, 1, step, peel=2)

        @block.scalar
        def _(act):
            act.preload_act_table_set("natural_log_exp_and_others")
            act.wait_ge(prep, 7)
            for b in range(B):
                g0 = b * NB

                def stage(t, gi, m):
                    par = ((t // PR) % 2) if isinstance(t, int) else (t // PR) % 2
                    act.wait_ge(x_in, (t // PR) * 16 + (16 + 16 * (H // BS) * b))
                    src = xs[:, bass.ds(par, 1), :, bass.ds((t % PR) * BS, BS)]
                    nc.scalar.activation(g[0:C, m].rearrange("c (o r w) -> c o r w", o=1, w=BS), src, ACT.Identity,
                                         bias=e.shift1[:, b:b + 1], scale=e.gain1[:, b:b + 1]).then_inc(S["g_sb"], 1)

                def square(gi, m, u):
                    w, f, h = project(gi, u)
                    after(act, S["p_mm"], UN, gi, u + 1)
                    nc.scalar.activation(fsq[:, m, f, h * T:(h + 1) * T], ps_p[:, u % 2, :], ACT.Square).then_inc(S["f_sq"], 1)

                def turned(gi, m, r):
                    after(act, S["gt_mm"], 2, gi, r + 1)
                    nc.scalar.copy(gt[:, m, 4 * r:4 * r + 4, :], ps_gt[:, :, 0:K1]).then_inc(S["gt_sb"], 1)

                def step(t, m, has):
                    i = t + g0
                    A, Bk, Ck = has(t + 1), has(t), has(t - 1)
                    n = (m + 1) % U
                    if A:
                        after(act, S["dn_mm"], 1, i - 1, 1)
                        square(i + 1, n, 0)
                    if Bk:
                        after(act, S["c2_max"], 1, i, 1)
                        nc.scalar.activation(rcn[:], n2c[:], ACT.Ln, scale=SC).then_inc(S["logged"], 1)
                        after(act, S["logged"], 2, i, 1)
                        nc.scalar.activation(rcn[:], rcn[:], ACT.Exp, bias=lnsc[:], scale=-0.5).then_inc(S["rcn_sb"], 1)
                    if A:
                        square(i + 1, n, 1)
                    if Ck:
                        after(act, S["m1"], 1, i - 1, 1)
                        nc.scalar.activation(sel[:], best[:], ACT.Exp, scale=-1.0).then_inc(S["e_sb"], 1)
                    if Bk:
                        turned(i, m, 0)
                    if A:
                        square(i + 1, n, 2)
                    if Bk:
                        after(act, S["d_mm"], 1, i, 1)
                        nc.scalar.copy(dsb[:], ps_s[0:K1, 0:HM]).then_inc(S["d_sb"], 1)
                    if A:
                        square(i + 1, n, 3)
                    if Bk:
                        turned(i, m, 1)
                    if Ck:
                        after(act, S["sc_mm"], 1, i - 1, 1)
                        nc.scalar.copy(simc[:], ps_st[:, 1, :]).then_inc(S["sc_sb"], 1)
                    if Bk:
                        after(act, S["n_max"], 1, i, 1)
                        nc.scalar.activation(rn[:], rn[:], ACT.Ln, scale=SC).then_inc(S["logged"], 1)
                        after(act, S["logged"], 2, i, 2)
                        nc.scalar.activation(rn[:], rn[:], ACT.Exp, bias=lnsc[:], scale=-0.5).then_inc(S["n_rn"], 1)
                    if Ck:
                        after(act, S["agg_mm"], 1, i - 1, 1)
                        nc.scalar.copy(agg[:], ps_s[0:HM, 0:K1 + 1]).then_inc(S["agg_sb"], 1)
                    if Ck:
                        after(act, S["at_mm"], 1, i - 1, 1)
                        nc.scalar.copy(aggt[:], ps_s[0:K1, 0:HM]).then_inc(S["at_sb"], 1)
                    if has(t + 2):
                        after(act, S["gt_mm"], 2, i, 2)
                        stage(t + 2, i + 2, m)
                    if Ck:
                        after(act, S["gg_mm"], 1, i - 1, 1)
                        after(act, S["rc_sb"], 1, i - 1, 1)
                        after(act, S["o_mm"], 2, i - 1)
                        for q in range(Q):
                            last = nc.scalar.activation(gbd[q * HM:(q + 1) * HM, q, :], ps_s[0:HM, 0:C], ACT.Copy, scale=rc[:])
                        last.then_inc(S["gbd_sb"], 1)
                pipeline(act, NB, U, 2, 1, step)

        @block.vector
        def _(dve):
            for x in (g[C:K1], ):
                nc.vector.memset(x, 1.0).then_inc(prep, 1)
            nc.vector.memset(onesb[:], 1.0).then_inc(prep, 1)
            nc.vector.memset(gbd[:], 0.0).then_inc(prep, 1)
            nc.vector.memset(lnsc[:], float(0.5 * np.log(SC))).then_inc(prep, 1)
            dve.wait_ge(w_in, 13 * 16)
            dve.wait_ge(prep_mm, 1)
            nc.vector.tensor_copy(wft[:].rearrange("k (f c) -> k f c", f=F), ps_gt[0:K1, 0:2, :]).then_inc(prep, 1)
            nc.vector.tensor_copy(wvt[:].rearrange("k (f c) -> k f c", f=F), ps_gt[0:K1, 2:4, :]).then_inc(prep, 1)
            nc.vector.tensor_copy(wpt[:].rearrange("c f k -> c (f k)"), ps_s[:, 0:F * C]).then_inc(prep, 1)
            dve.wait_ge(prep, 7)
            for b in range(B):
                g0 = b * NB

                def pool_max(gi, m, u):
                    w, f, h = project(gi, u)
                    if u < 4:
                        after(dve, S["f_sq"], 4, gi, u + 1)
                    after(dve, S["p_mm"], UN, gi, u + 1)
                    dst = fc if u < 4 else vc
                    nc.vector.tensor_reduce(dst[:, m, f, 2 * h:2 * h + 2],
                                            ps_p[:, u % 2, :].rearrange("p (r k c) -> p k r c", k=2, c=BS // 2),
                                            AX.XY, ALU.max).then_inc(S["pooled"], 1)

                def step(t, m, has):
                    i = t + g0
                    A, Bk, Ck = has(t + 1), has(t), has(t - 1)
                    n = (m + 1) % U
                    if Bk:
                        after(dve, S["c2_mm"], 1, i, 1)
                        nc.vector.tensor_scalar(n2c[:], ps_s[:, 0:F * NC1], TINY, None, ALU.max).then_inc(S["c2_max"], 1)
                    if A:
                        pool_max(i + 1, n, 0)
                    if Ck:
                        after(dve, S["st_mm"], 1, i - 1, 1)
                        after(dve, S["agg_mm"], 1, i - 1)
                        st = ps_st[:, 0, :].rearrange("p (g m) -> p g m", m=NC1)
                        bb = best[:].unsqueeze(2).to_broadcast([P, 2 * Q * H1, NC1])
                        nc.vector.tensor_reduce(best[:], st, AX.X, ALU.max).then_inc(S["m1"], 1)
                        after(dve, S["m1"], 1, i - 1, 1)
                        nc.vector.tensor_tensor(win[:], st, bb, ALU.is_ge).then_inc(S["won"], 1)
                    if A:
                        pool_max(i + 1, n, 1)
                    if Bk:
                        after(dve, S["rcn_sb"], 1, i, 1)
                        nc.vector.tensor_tensor(nwt[:], rcn[:], n2c[:], ALU.mult).then_inc(S["newton"], 1)
                        after(dve, S["newton"], 3, i, 1)
                        nc.vector.scalar_tensor_tensor(out=nwt2[:], in0=nwt[:], scalar=-0.5, in1=rcn[:],
                                                       op0=ALU.mult, op1=ALU.mult).then_inc(S["newton"], 1)
                        after(dve, S["newton"], 3, i, 2)
                        nc.vector.scalar_tensor_tensor(out=nwt[:], in0=nwt2[:], scalar=1.5, in1=rcn[:],
                                                       op0=ALU.add, op1=ALU.mult).then_inc(S["newton"], 1)
                        after(dve, S["newton"], 3, i, 3)
                        nc.vector.tensor_tensor(cn[:], fc[:, m].rearrange("p f k -> p (f k)"), nwt[:], ALU.mult).then_inc(S["cn_sb"], 1)
                        after(dve, S["cn_sb"], 1, i, 1)
                        cnv = cn[:].rearrange("p (f k) -> p f k", f=F)
                        for f in range(F):
                            last = nc.vector.tensor_tensor(cnbd[:, f].rearrange("p (h m) -> p h m", m=NC1),
                                                           headc[:, f].rearrange("p (h m) -> p h m", m=NC1),
                                                           cnv[:, f].unsqueeze(1).to_broadcast([P, H1, NC1]), ALU.mult)
                        last.then_inc(S["cnbd_sb"], 1)
                    if Ck:
                        after(dve, S["won"], 3, i - 1, 1)
                        nc.vector.tensor_tensor(win[:], win[:], first[:], ALU.mult).then_inc(S["won"], 1)
                        after(dve, S["won"], 3, i - 1, 2)
                        nc.vector.tensor_reduce(lead[:], win[:], AX.X, ALU.max).then_inc(S["won"], 1)
                        after(dve, S["e_sb"], 1, i - 1, 1)
                        nc.vector.tensor_scalar(sel1[:], sel[:], 1.0, None, ALU.add).then_inc(S["e1_sb"], 1)
                        after(dve, S["won"], 3, i - 1, 3)
                        nc.vector.tensor_tensor(mask[:], win[:], lead[:].unsqueeze(2).to_broadcast([P, 2 * Q * H1, NC1]),
                                                ALU.is_equal).then_inc(S["m5"], 1)
                        after(dve, S["e1_sb"], 1, i - 1, 1)
                        nc.vector.reciprocal(seln[:], sel1[:]).then_inc(S["sim_sb"], 1)
                        after(dve, S["sim_sb"], 1, i - 1, 1)
                        after(dve, S["m5"], 1, i - 1, 1)
                        nc.vector.tensor_tensor(simm[:].rearrange("p a (g m) -> p (a g) m", m=NC1), mask[:],
                                                seln[:].unsqueeze(2).to_broadcast([P, 2 * Q * H1, NC1]),
                                                ALU.mult).then_inc(S["simm_sb"], 1)
                    if A:
                        pool_max(i + 1, n, 2)
                    if A:
                        pool_max(i + 1, n, 3)
                    if A:
                        after(dve, S["pooled"], UN, i + 1, 4)
                        after(dve, S["c2_mm"], 1, i, 1)
                        nc.vector.tensor_tensor(fcs[:], fc[:, n].rearrange("p f k -> p (f k)"),
                                                fc[:, n].rearrange("p f k -> p (f k)"), ALU.mult).then_inc(S["fcs_sb"], 1)
                    if Bk:
                        after(dve, S["dn_mm"], 1, i, 1)
                        after(dve, S["cos_sb"], 1, i)
                        nc.vector.tensor_scalar(rn[:], ps_dn[:, 0, :], TINY, None, ALU.max).then_inc(S["n_max"], 1)
                    if Bk:
                        after(dve, S["pooled"], UN, i, UN)
                        nc.vector.tensor_copy(vcb[:, m], vc[:, m])
                    if A:
                        pool_max(i + 1, n, 4)
                    if Bk:
                        after(dve, S["n_rn"], 1, i, 1)
                        nc.vector.tensor_tensor(cos[:], ps_dn[:, 1, :], rn[:], ALU.mult).then_inc(S["cos_sb"], 1)
                    if Ck:
                        after(dve, S["agg_sb"], 1, i - 1, 1)
                        nc.vector.tensor_scalar(cnt[:], agg[:, K1:K1 + 1], 1.0, None, ALU.add).then_inc(S["cnt_sb"], 1)
                        after(dve, S["cnt_sb"], 1, i - 1, 1)
                        nc.vector.reciprocal(rc[:], cnt[:]).then_inc(S["rc_sb"], 1)
                    if A:
                        pool_max(i + 1, n, 5)
                    if Ck:
                        after(dve, S["av_mm"], 1, i - 1, 1)
                        for f in range(F):
                            last = nc.vector.tensor_tensor(num[:, f].rearrange("p (h m) -> p h m", m=NC1),
                                                           ps_s[:, f * HM:(f + 1) * HM].rearrange("p (h m) -> p h m", m=NC1),
                                                           vcb[:, n, f].unsqueeze(1).to_broadcast([P, H1, NC1]), ALU.add)
                        last.then_inc(S["nums"], 1)
                        after(dve, S["nums"], 2, i - 1, 1)
                        nc.vector.tensor_tensor(num[:], num[:], headc[:], ALU.mult).then_inc(S["nums"], 1)
                    if A:
                        pool_max(i + 1, n, 6)
                    if Bk:
                        after(dve, S["cos_sb"], 1, i, 1)
                        nc.vector.tensor_scalar(cos[:], cos[:], alpha[:], beta[:], ALU.mult, ALU.add).then_inc(S["zs"], 1)
                        after(dve, S["zs"], 2, i, 1)
                        nc.vector.tensor_scalar(z[:, m], cos[:], ZMAX, ZMIN, ALU.min, ALU.max).then_inc(S["zs"], 1)
                    if A:
                        pool_max(i + 1, n, 7)
                    if Ck:
                        tt = t - 1
                        for h in range(2):
                            after(dve, S["o_mm"], 2, i - 1, h + 1)
                            xv = xs[:, bass.ds((tt // PR) % 2, 1), h * HP:(h + 1) * HP, bass.ds((tt % PR) * BS, BS)]
                            nc.vector.scalar_tensor_tensor(out=xv, in0=ps_o[:, h, :].rearrange("c (o r w) -> c o r w", o=1, w=BS),
                                                           scalar=bp[:], in1=xv, op0=ALU.add, op1=ALU.add).then_inc(S["o_done"], 1)
                pipeline(dve, NB, U, 1, 1, step)


def build(nc, aps, out):
    e = Env()
    e.x = aps["x"].rearrange("b c h w -> b c (h w)")
    e.out = out.rearrange("b c h w -> b c (h w)")
    e.aps = aps

    def dram(name, shape):
        return nc.dram_tensor(name, shape, F32, kind="Internal").ap()

    e.y = dram("y_normed", (B, C, HW))
    e.attn = dram("attended", (B, C, HW))
    e.hid = dram("hidden", (MLP, B, H, WP))
    e.tab = dram("taps_padded", (MLP, KS, TAB))
    e.z = dram("hidden_sum", (MLP, B, HW))
    e.x1 = dram("x1", (B, C, HW))
    with ExitStack() as ctx:
        def sb(name, shape, dt=F32):
            return ctx.enter_context(nc.sbuf_tensor(name, shape, dt))
        e.groups = sb("groups", [C, C])
        e.centre = sb("centre", [C, C])
        e.mean = sb("mean", [C, C])
        e.ident = sb("ident", [P, P])
        e.eps = sb("eps", [P, 1])
        e.gain0, e.shift0 = sb("gain0", [C, B]), sb("shift0", [C, B])
        e.gain1, e.shift1 = sb("gain1", [C, B]), sb("shift1", [C, B])
        consts = ctx.enter_context(nc.semaphore("consts"))
        e.passed = ctx.enter_context(nc.semaphore("passed"))
        with nc.Block() as block:
            @block.sync
            def _(sp):
                for t, name in ((e.groups, "c_groups"), (e.centre, "c_centre"), (e.mean, "c_mean"), (e.ident, "c_ident")):
                    sp.dma_start(t[:], aps[name]).then_inc(consts, 16)
                sp.wait_ge(consts, 4 * 16)

            @block.vector
            def _(dve):
                nc.vector.memset(e.eps[:], EPS)
        with nc.sbuf_tensor("moments0", [C, B * (HW // T) * 6], F32) as e.moments:
            stage_stats(nc, e, e.x, "stats0")
            stage_affine(nc, e, e.gain0, e.shift0, "affine0")
        stage_norm1(nc, e)
        stage_attend(nc, e)
        stage_expand(nc, e)
        stage_conv(nc, e)
        with nc.sbuf_tensor("moments1", [C, B * (HW // T) * 6], F32) as e.moments:
            stage_contract(nc, e)
            stage_affine(nc, e, e.gain1, e.shift1, "affine1")
        stage_cluster(nc, e)


_INS = ["x", "L0_conv_norm1_w", "L0_conv_norm1_b", "L0_conv_wq", "L0_conv_wk", "L0_conv_wv", "L0_conv_wproj",
        "L0_conv_norm2_w", "L0_conv_norm2_b", "L0_conv_fc1_w", "L0_conv_fc1_b", "L0_conv_dw_w", "L0_conv_dw_b",
        "L0_conv_fc2_w", "L0_conv_fc2_b", "L1_conv_Wf", "L1_conv_bf", "L1_conv_Wv", "L1_conv_bv", "L1_conv_Wp",
        "L1_conv_bp", "L1_conv_sim_alpha", "L1_conv_sim_beta"]


def kernel(**inputs):
    import concourse.bacc as _bacc
    from concourse.bass_utils import run_bass_kernel_spmd as _run

    nc = _bacc.Bacc("TRN2", target_bir_lowering=False, num_devices=1)
    arrays = {name: np.ascontiguousarray(inputs[name]) for name in _INS}
    arrays.update(constants())
    aps = {name: nc.dram_tensor(name, v.shape, mybir.dt.from_np(v.dtype), kind="ExternalInput").ap()
           for name, v in arrays.items()}
    out = nc.dram_tensor("out", (B, C, H, W), F32, kind="ExternalOutput").ap()
    build(nc, aps, out)
    r = _run(nc, [arrays], core_ids=[0])
    return r.results[0]["out"]
```
